# Optimizing a Trainium2 kernel written in Bass

```python
import numpy as np
import jax
import jax.numpy as jnp

def _softmax(x, axis=-1):
    return jax.nn.softmax(x, axis=axis)

def _gelu(x):
    return jax.nn.gelu(x, approximate=True)

def _silu(x):
    return jax.nn.silu(x)

def _sigmoid(x):
    return jax.nn.sigmoid(x)

def _layernorm(x, axis=-1, eps=1e-05):
    m = jnp.mean(x, axis=axis, keepdims=True)
    v = jnp.var(x, axis=axis, keepdims=True)
    return (x - m) / jnp.sqrt(v + eps)

def _scatter_add(tgt, idx, src, axis=0):
    return tgt.at[idx].add(src)

def _segment_sum(src, seg, n):
    return jax.ops.segment_sum(src, seg, n)
kernel_name = 'mk_recurrent_d1_jaxref_r8_b1c799'

def setup_inputs(seed: int=0):
    np.random.seed(seed)
    _w = jnp.asarray

    def _L0_attn_setup():
        import jax, jax.numpy as jnp
        import numpy as np
        SCALING = 1.0
        H, N = (128, 64)
        B, L = (4, 256)
        key = jax.random.key(seed)
        ks = jax.random.split(key, 10)
        x = jax.random.normal(ks[0], (B, L, H), dtype=jnp.float32)
        in_proj = jax.random.normal(ks[1], (H, N), dtype=jnp.float32)
        out_proj = jax.random.normal(ks[2], (N, H), dtype=jnp.float32)
        lo, hi = (np.log(0.01), np.log(100.0))
        frequencies = jnp.exp(jax.random.uniform(ks[3], (N,)) * (hi - lo) + lo) / SCALING
        decays = jnp.full((N,), np.log(0.5), dtype=jnp.float32)
        s = 1.0 / np.sqrt(H)
        ss_W = jax.random.uniform(ks[4], (H, H), minval=-s, maxval=s)
        ss_b = jax.random.uniform(ks[5], (H,), minval=-s, maxval=s)
        gate_W = jax.random.uniform(ks[6], (H, H), minval=-s, maxval=s)
        gate_b = jax.random.uniform(ks[7], (H,), minval=-s, maxval=s)
        fin_W = jax.random.uniform(ks[8], (H, H), minval=-s, maxval=s)
        fin_b = jax.random.uniform(ks[9], (H,), minval=-s, maxval=s)
        return {'x': x, 'in_proj': in_proj, 'out_proj': out_proj, 'frequencies': frequencies, 'decays': decays, 'ss_W': ss_W, 'ss_b': ss_b, 'gate_W': gate_W, 'gate_b': gate_b, 'fin_W': fin_W, 'fin_b': fin_b}
    _L0_attn_in = _L0_attn_setup()

    def _L0_ffn_setup():
        import jax, jax.numpy as jnp
        import numpy as np
        DIM = 128
        INTER = 64
        E = 8
        TOP_K = 2
        ROUTE_SCALE = 1.0
        key = jax.random.key(seed)
        ks = jax.random.split(key, 8)
        s_d = 1.0 / np.sqrt(DIM)
        s_f = 1.0 / np.sqrt(INTER)
        x = jax.random.normal(ks[0], (2, 256, DIM), dtype=jnp.float32)
        gate_w = jax.random.uniform(ks[1], (E, DIM), jnp.float32, -s_d, s_d)
        wg = jax.random.uniform(ks[2], (E, INTER, DIM), jnp.float32, -s_d, s_d)
        wu = jax.random.uniform(ks[3], (E, INTER, DIM), jnp.float32, -s_d, s_d)
        wd = jax.random.uniform(ks[4], (E, DIM, INTER), jnp.float32, -s_f, s_f)
        sg = jax.random.uniform(ks[5], (INTER, DIM), jnp.float32, -s_d, s_d)
        su = jax.random.uniform(ks[6], (INTER, DIM), jnp.float32, -s_d, s_d)
        sd = jax.random.uniform(ks[7], (DIM, INTER), jnp.float32, -s_f, s_f)
        return {'x': x, 'gate_w': gate_w, 'wg': wg, 'wu': wu, 'wd': wd, 'sg': sg, 'su': su, 'sd': sd}
    _L0_ffn_in = _L0_ffn_setup()
    _d = {'L0_attn_x': _L0_attn_in['x'], 'L0_attn_in_proj': _L0_attn_in['in_proj'], 'L0_attn_out_proj': _L0_attn_in['out_proj'], 'L0_attn_frequencies': _L0_attn_in['frequencies'], 'L0_attn_decays': _L0_attn_in['decays'], 'L0_attn_ss_W': _L0_attn_in['ss_W'], 'L0_attn_ss_b': _L0_attn_in['ss_b'], 'L0_attn_gate_W': _L0_attn_in['gate_W'], 'L0_attn_gate_b': _L0_attn_in['gate_b'], 'L0_attn_fin_W': _L0_attn_in['fin_W'], 'L0_attn_fin_b': _L0_attn_in['fin_b'], 'L0_ffn_gate_w': _L0_ffn_in['gate_w'], 'L0_ffn_wg': _L0_ffn_in['wg'], 'L0_ffn_wu': _L0_ffn_in['wu'], 'L0_ffn_wd': _L0_ffn_in['wd'], 'L0_ffn_sg': _L0_ffn_in['sg'], 'L0_ffn_su': _L0_ffn_in['su'], 'L0_ffn_sd': _L0_ffn_in['sd']}
    _x0 = _d['L0_attn_x']
    _d['L0_attn_x'] = jax.random.normal(jax.random.fold_in(jax.random.key(seed), 1), (8, 512, 128), dtype=_x0.dtype)
    del _x0
    return _d

def reference(L0_attn_x, L0_attn_in_proj, L0_attn_out_proj, L0_attn_frequencies, L0_attn_decays, L0_attn_ss_W, L0_attn_ss_b, L0_attn_gate_W, L0_attn_gate_b, L0_attn_fin_W, L0_attn_fin_b, L0_ffn_gate_w, L0_ffn_wg, L0_ffn_wu, L0_ffn_wd, L0_ffn_sg, L0_ffn_su, L0_ffn_sd):

    def _L0_attn_ref(x, in_proj, out_proj, frequencies, decays, ss_W, ss_b, gate_W, gate_b, fin_W, fin_b):
        import jax, jax.numpy as jnp
        import numpy as np
        SCALING = 1.0
        B, L, H = x.shape
        fft_len = 2 * L - 1
        freqs = frequencies * (2.0 * jnp.pi * SCALING)
        dec = -jnp.exp(decays) * SCALING
        lam = dec + 1j * freqs
        kernel = jnp.exp(lam[None, :] * jnp.arange(L, dtype=jnp.float32)[:, None])
        k = jnp.einsum('hn,kn,nh->hk', in_proj.astype(kernel.dtype), kernel, out_proj.astype(kernel.dtype)).real
        u = jnp.transpose(x, (0, 2, 1))
        u_f = jnp.fft.fft(u, n=fft_len, axis=-1)
        k_f = jnp.fft.fft(k, n=fft_len, axis=-1)
        conv = jnp.fft.ifft(u_f * k_f[None], axis=-1)[:, :, :L].real
        ss_out = jnp.transpose(conv, (0, 2, 1))
        ss_out = jax.nn.gelu(ss_out @ ss_W.T + ss_b, approximate=False)
        gate = jax.nn.gelu(x @ gate_W.T + gate_b, approximate=False)
        return gate * ss_out @ fin_W.T + fin_b

    def _L0_ffn_ref(x, gate_w, wg, wu, wd, sg, su, sd):
        import jax, jax.numpy as jnp
        import numpy as np
        DIM = 128
        INTER = 64
        E = 8
        TOP_K = 2
        ROUTE_SCALE = 1.0
        B, S, D = x.shape
        xf = x.reshape(-1, D)
        N = xf.shape[0]
        scores = jax.nn.softmax(xf @ gate_w.T, axis=-1)
        _, idx = jax.lax.top_k(scores, TOP_K)
        weights = jnp.take_along_axis(scores, idx, axis=-1) * ROUTE_SCALE
        cw = jnp.zeros((N, E), dtype=xf.dtype)
        cw = cw.at[jnp.arange(N)[:, None], idx].add(weights)
        g = jnp.einsum('nd,efd->nef', xf, wg)
        u = jnp.einsum('nd,efd->nef', xf, wu)
        h = jax.nn.silu(g) * u
        y = jnp.einsum('nef,edf->ned', h, wd)
        routed = jnp.einsum('ned,ne->nd', y, cw)
        shared = jax.nn.silu(xf @ sg.T) * (xf @ su.T) @ sd.T
        return (routed + shared).reshape(B, S, D)
    x = L0_attn_x
    xn = _layernorm(x, axis=-1)
    s = _L0_attn_ref(xn, L0_attn_in_proj, L0_attn_out_proj, L0_attn_frequencies, L0_attn_decays, L0_attn_ss_W, L0_attn_ss_b, L0_attn_gate_W, L0_attn_gate_b, L0_attn_fin_W, L0_attn_fin_b)
    g = _silu(_L0_ffn_ref(xn, L0_ffn_gate_w, L0_ffn_wg, L0_ffn_wu, L0_ffn_wd, L0_ffn_sg, L0_ffn_su, L0_ffn_sd))
    x = x + s * g
    return x

_drawn_inputs = setup_inputs


def setup_inputs(seed=0):
    import zlib

    import numpy as np

    out = dict(_drawn_inputs(seed))
    spreads = {'L0_attn_decays': (-0.6931471824645996, 0.6)}
    factors = {'L0_attn_frequencies': 3.07,
     'L0_attn_ss_b': 8.0,
     'L0_attn_gate_b': 8.0,
     'L0_attn_fin_b': 8.0,
     'L0_ffn_gate_w': 5.264,
     'L0_ffn_wg': 4.724,
     'L0_ffn_wu': 4.603,
     'L0_ffn_wd': 4.634,
     'L0_ffn_sg': 5.575,
     'L0_ffn_su': 5.472,
     'L0_ffn_sd': 5.471}
    for name, (base, spread) in spreads.items():
        noise = np.random.default_rng([zlib.crc32(name.encode()), seed]).standard_normal(out[name].shape)
        drawn = base * np.exp(spread * noise) if base else spread * noise
        out[name] = jnp.asarray(drawn.astype(out[name].dtype))
    for name, factor in factors.items():
        out[name] = (out[name] * factor).astype(out[name].dtype)
    return out
```

```python
from contextlib import ExitStack

import numpy as np

import concourse.bass as bass
from concourse import mybir

F32 = mybir.dt.float32
F32R = mybir.dt.float32r
BF16 = mybir.dt.bfloat16
I32 = mybir.dt.int32
ALU = mybir.AluOpType
ACT = mybir.ActivationFunctionType
AX = mybir.AxisListType.X

P = 128
B, L, H = 8, 512, 128
C = L // P
NT = B * C
N = 64
E, F = 8, 64
EPS = 1e-5
PAIRS = E // 2
BLOCKS = PAIRS + 1
SHARED = PAIRS
GU = 2 * PAIRS + 1
RING = 3
CH = 16

def columns(*parts):
    at, out = 0, {}
    for name, width in parts:
        out[name] = (at, width)
        at += width
    return out, at


MODE_COLS, MODE_W = columns(("freq", 1), ("decay", 1), ("sign", 1), ("in", H), ("out", H))
EARLY_COLS, EARLY_W = columns(("ident", P), ("router", E))
WIDE_COLS, WIDE_W = columns(("gu", GU * P), ("gate", H))
LATE_COLS, LATE_W = columns(("wd", BLOCKS * H), ("ss", H), ("fin", H), ("ss_b", 1), ("gate_b", 1))

TWO_PI = 6.283185307179586
TP1 = 6.25
TP2 = 17.0 / 512.0
TP3 = TWO_PI - TP1 - TP2
ROUND = 1.5 * 2.0 ** 23
PI_BELOW = 3.1415925
BIG = 3.0e38

FWD = P + 1
REV = (C - 1) * P
TAB = FWD + REV


def layer(nc, x, modes, early, wide, late, fin_b, ident_bf, select, out):
    ctx = ExitStack()
    with ctx:
        def sb(name, shape, dt=F32):
            return ctx.enter_context(nc.sbuf_tensor(name, shape, dt))

        def sem(name):
            return ctx.enter_context(nc.semaphore(name))

        x_tok = sb("x_tok", [P, B, C, H])
        modes_sb = sb("modes_sb", [P, MODE_W])
        early_sb = sb("early_sb", [P, EARLY_W])
        wide_sb = sb("wide_sb", [P, WIDE_W])
        late_sb = sb("late_sb", [P, LATE_W])
        fin_b_sb = sb("fin_b_sb", [P, H])
        ident16 = sb("ident16", [P, P], BF16)
        select_sb = sb("select_sb", [P, PAIRS, C, P], BF16)
        wide_hi = sb("wide_hi", [P, WIDE_W], F32R)
        wide_lo = sb("wide_lo", [P, WIDE_W], F32R)

        def part(t, cols, name):
            at, width = cols[name]
            return t[:, at:at + width]

        freq = part(modes_sb, MODE_COLS, "freq")
        decay = part(modes_sb, MODE_COLS, "decay")
        sign = part(modes_sb, MODE_COLS, "sign")
        ident = part(early_sb, EARLY_COLS, "ident")
        router = part(early_sb, EARLY_COLS, "router")
        wd = part(late_sb, LATE_COLS, "wd").rearrange("p (j d) -> p j d", j=BLOCKS)
        ss_w = part(late_sb, LATE_COLS, "ss")
        fin_w = part(late_sb, LATE_COLS, "fin")
        ss_b = part(late_sb, LATE_COLS, "ss_b")
        gate_b = part(late_sb, LATE_COLS, "gate_b")

        def gu(t, block):
            return t[:, block * P:(block + 1) * P]

        gate_at = WIDE_COLS["gate"][0]

        stats = sb("stats", [P, NT, 6])
        moments = sb("moments", [P, NT, 2])
        eps = sb("eps", [P, 1])
        half_pi = sb("half_pi", [P, 1])
        std = sb("std", [P, NT])
        rstd = sb("rstd", [P, NT])
        xn = sb("xn", [P, B, C, H])
        xt_full = sb("xt_full", [P, 2, L])
        xt_hi = sb("xt_hi", [P, B, L], F32R)
        xt_lo = sb("xt_lo", [P, B, L], F32R)

        rank = sb("rank", [P, NT, E])
        ranki = sb("ranki", [P, NT, E], I32)
        top = sb("top", [P, NT])
        below = sb("below", [P, NT, E])
        expd = sb("expd", [P, NT, E])
        total = sb("total", [P, NT])
        rtotal = sb("rtotal", [P, NT])
        key = sb("key", [P, NT, E])
        best = sb("best", [P, NT])
        first = sb("first", [P, NT, E])
        rest = sb("rest", [P, NT, E])
        second = sb("second", [P, NT, E])
        weight = sb("weight", [P, NT, E])
        remain = sb("remain", [P, NT, E])
        parts = sb("parts", [P, NT, 4, E], BF16)
        weight_t = sb("weight_t", [P, B, P], BF16)

        omega = sb("omega", [P, 1])
        rate = sb("rate", [P, 1])
        steps = sb("steps", [P, TAB], I32)
        phase = sb("phase", [P, TAB])
        amp = sb("amp", [P, TAB])
        trig = sb("trig", [P, TAB])
        turns = trig
        table = sb("table", [P, TAB])
        mix = sb("mix", [P, H])
        mix_signed = sb("mix_signed", [P, H])
        decay_t = sb("decay_t", [P, C - 1, P])
        kpad = sb("kpad", [P, 2 * P])
        toeplitz = sb("toeplitz", [P, RING, CH, P])
        inside = sb("inside", [P, 2, 4, P])
        state = sb("state", [P, C - 1, B, H])
        conv = sb("conv", [P, B, C, P])

        act_g = sb("act_g", [P, 2, L])
        prod = sb("prod", [P, 2, L])
        hidden = sb("hidden", [P, 2, L])
        g_all = sb("g_all", [P, B, L])
        gated, ssg, both = act_g, prod, hidden
        s_sum, s_g, y_out = (toeplitz[:, i, 0:8, :].rearrange("p (n r) i -> p n (r i)", n=2) for i in range(3))

        k_dram = nc.dram_tensor("k_dram", (P, 2 * P), F32, kind="Internal").ap()

        conv_dram = nc.dram_tensor("conv_dram", (H, NT, P), F32, kind="Internal").ap()

        def bank(name):
            return ctx.enter_context(nc.psum_tensor(name, [P, L], F32))

        ps_g = [bank("ps_g0"), bank("ps_g1")]
        ps_u = [bank("ps_u0"), bank("ps_u1")]
        ps_w = bank("ps_w")
        ps_side = bank("ps_side")
        ps_o = [bank("ps_o0"), bank("ps_o1")]
        ps_x, ps_logit = ps_g, ps_u[0]
        ps_gate, ps_inter, ps_ss, ps_fin = ps_g, ps_u, [ps_w, ps_side], ps_o
        ps_w16 = ps_w[:, :].bitcast(BF16)

        x_loaded = [sem(f"x_loaded{b}") for b in range(B)]
        modes_loaded, early_loaded = sem("modes_loaded"), sem("early_loaded")
        wide_loaded, late_loaded = sem("wide_loaded"), sem("late_loaded")
        select_loaded = sem("select_loaded")
        consts_ready, steps_ready, rank_ready = sem("consts_ready"), sem("steps_ready"), sem("rank_ready")
        stats_ready, moments_ready, std_ready = sem("stats_ready"), sem("moments_ready"), sem("std_ready")
        rstd_ready, xn_ready = sem("rstd_ready"), sem("xn_ready")
        xt_psum, xt_full_ready, xt_hi_ready, xt_lo_ready = (
            sem("xt_psum"), sem("xt_full_ready"), sem("xt_hi_ready"), sem("xt_lo_ready"))
        wide_hi_ready, wide_lo_ready = sem("wide_hi_ready"), sem("wide_lo_ready")
        logits_psum, below_ready, expd_ready = sem("logits_psum"), sem("below_ready"), sem("expd_ready")
        route, mode = sem("route"), sem("mode")
        parts_ready, weight_psum, weight_t_ready = sem("parts_ready"), sem("weight_psum"), sem("weight_t_ready")
        rate_ready, amp_ready, angle_ready, trig_ready = (
            sem("rate_ready"), sem("amp_ready"), sem("angle_ready"), sem("trig_ready"))
        decay_exp_ready = sem("decay_exp_ready")
        mix_ready, table_ready, taps_psum = sem("mix_ready"), sem("table_ready"), sem("taps_psum")
        kpad_ready, decay_t_ready, k_stored = sem("kpad_ready"), sem("decay_t_ready"), sem("k_stored")
        toeplitz_loaded = [sem(f"toeplitz_loaded{i}") for i in range(RING)]
        up_psum, act_g_ready, prod_ready = sem("up_psum"), sem("act_g_ready"), sem("prod_ready")
        bcast_psum, hidden_ready, down_psum = sem("bcast_psum"), sem("hidden_ready"), sem("down_psum")
        g_ready = sem("g_ready")
        inside_psum, inside_ready = sem("inside_psum"), sem("inside_ready")
        conv_loaded = [sem(f"conv_loaded{b}") for b in range(B)]
        inside_moved = [sem(f"inside_moved{i}") for i in range(2)]
        state_psum, state_ready = sem("state_psum"), sem("state_ready")
        gate_psum, gate_ready, inter_psum, conv_ready = (
            sem("gate_psum"), sem("gate_ready"), sem("inter_psum"), sem("conv_ready"))
        ss_psum, ssg_ready, both_ready = sem("ss_psum"), sem("ssg_ready"), sem("both_ready")
        fin_psum, s_sum_ready, s_g_ready, y_ready = (
            sem("fin_psum"), sem("s_sum_ready"), sem("s_g_ready"), sem("y_ready"))
        y_stored = [sem(f"y_stored{i}") for i in range(2)]

        STEPS = B * BLOCKS

        def routed_steps(s):
            return s // BLOCKS * PAIRS + min(s % BLOCKS, PAIRS)

        STATES = [(c, half) for c in range(1, C) for half in range(2)]
        side = {BLOCKS - 1: ("taps", 0)}
        for b in range(1, B):
            side[b * BLOCKS + 1] = ("inside", b - 1)
            side[b * BLOCKS + 3] = ("state", b - 1) if b < B - 1 else ("inside", B - 1)
        side_order = [side[s] for s in sorted(side)]

        def side_free(eng, s):
            n = side_order.index(side[s])
            if n == 0:
                return
            kind, i = side_order[n - 1]
            if kind == "taps":
                eng.wait_ge(kpad_ready, 2)
                eng.wait_ge(decay_t_ready, 1)
            elif kind == "inside":
                eng.wait_ge(inside_ready, i + 1)
            else:
                eng.wait_ge(state_ready, i + 1)

        block = ctx.enter_context(nc.Block())

        @block.sync
        def _(sp):
            sp.dma_start(modes_sb[:, :], modes).then_inc(modes_loaded, 16)
            for b in range(B):
                sp.dma_start(x_tok[:, b], x[b].rearrange("(c j) h -> j c h", j=P)).then_inc(x_loaded[b], 16)
            sp.wait_ge(kpad_ready, 2)
            sp.dma_start(k_dram, kpad[:, :]).then_inc(k_stored, 16)
            sp.wait_ge(k_stored, 16)

            def load_toeplitz(k):
                if k >= RING:
                    sp.wait_ge(inside_psum, k - RING + 1)
                src = bass.AP(k_dram.tensor, k_dram.offset + k * CH * 2 * P, [[1, P], [2 * P, CH], [1, P]])
                sp.dma_start(toeplitz[:, k % RING], src).then_inc(toeplitz_loaded[k % RING], 16)

            for k in range(RING):
                load_toeplitz(k)
            for k in range(B):
                sp.wait_ge(inside_ready, k + 1)
                sp.dma_start(conv_dram[k * CH:(k + 1) * CH].rearrange("(r q) m i -> (q m) r i", q=4),
                             inside[:, k % 2, :, :]).then_inc(inside_moved[k % 2], 16)
                if k + RING < B:
                    load_toeplitz(k + RING)
            for i in range(2):
                sp.wait_ge(inside_moved[i], 16 * (B // 2))
            for b in range(B):
                sp.dma_start(conv[:, b, :, :], conv_dram[:, b * C:(b + 1) * C, :]).then_inc(conv_loaded[b], 16)
            for b in range(B):
                sp.wait_ge(y_ready, b + 1)
                sp.dma_start(out[b].rearrange("(c j) h -> j c h", j=P),
                             y_out[:, b % 2, :].rearrange("j (c h) -> j c h", c=C)).then_inc(y_stored[b % 2], 16)
            for i in range(2):
                sp.wait_ge(y_stored[i], 16 * (B // 2))

        @block.gpsimd
        def _(pool):
            pool.memset(eps[:, :], EPS).then_inc(consts_ready, 1)
            pool.memset(half_pi[:, :], TWO_PI / 4).then_inc(consts_ready, 1)
            pool.iota(steps[:, 0:FWD], [[1, FWD]], base=0, channel_multiplier=0).then_inc(steps_ready, 1)
            pool.iota(steps[:, FWD:TAB], [[-1, REV]], base=REV - 1, channel_multiplier=0).then_inc(steps_ready, 1)
            pool.iota(ranki[:, :, :], [[0, NT], [-1, E]], base=E, channel_multiplier=0).then_inc(rank_ready, 1)
            pool.memset(kpad[:, :], 0.0).then_inc(kpad_ready, 1)
            pool.memset(parts[:, :, 3, :], 0.0).then_inc(parts_ready, 1)
            pool.wait_ge(wide_loaded, 16)
            pool.tensor_copy(wide_hi[:, :], wide_sb[:, :]).then_inc(wide_hi_ready, 1)
            pool.wait_ge(wide_hi_ready, 1)
            pool.tensor_tensor(wide_lo[:, :], wide_sb[:, :], wide_hi[:, :].bitcast(F32),
                               ALU.subtract).then_inc(wide_lo_ready, 1)
            for b in range(B):
                pool.wait_ge(xt_full_ready, b + 1)
                pool.wait_ge(xt_hi_ready, b + 1)
                pool.tensor_tensor(xt_lo[:, b, :], xt_full[:, b % 2, :], xt_hi[:, b, :].bitcast(F32),
                                   ALU.subtract).then_inc(xt_lo_ready, 1)
            for b in range(B):
                pool.wait_ge(s_g_ready, b + 1)
                if b >= 2:
                    pool.wait_ge(y_stored[b % 2], 16 * (b // 2))
                pool.tensor_tensor(y_out[:, b % 2, :], s_g[:, b % 2, :],
                                   x_tok[:, b].rearrange("j c h -> j (c h)"), ALU.add).then_inc(y_ready, 1)

        @block.scalar
        def _(act):
            act.dma_start(early_sb[:, :], early).then_inc(early_loaded, 16)
            act.dma_start(wide_sb[:, :], wide).then_inc(wide_loaded, 16)
            act.dma_start(late_sb[:, :], late).then_inc(late_loaded, 16)
            act.dma_start(ident16[:, :], ident_bf).then_inc(select_loaded, 16)
            act.dma_start(select_sb[:, :, :, :], select).then_inc(select_loaded, 16)
            act.dma_start(fin_b_sb[:, :], fin_b.partition_broadcast(P)).then_inc(late_loaded, 16)
            act.wait_ge(modes_loaded, 16)
            act.activation(rate[:, :], decay, ACT.Exp).then_inc(decay_exp_ready, 1)
            act.wait_ge(rate_ready, 1)
            act.wait_ge(steps_ready, 2)
            act.activation(amp[:, :], steps[:, :], ACT.Exp, scale=rate[:, 0:1]).then_inc(amp_ready, 1)
            act.wait_ge(consts_ready, 2)

            def take_transposed(b):
                act.wait_ge(xt_psum, b + 1)
                if b >= 2:
                    act.wait_ge(logits_psum, b - 1)
                    act.wait_ge(xt_lo_ready, b - 1)
                act.copy(xt_full[:, b % 2, :], ps_x[b % 2][:, :]).then_inc(xt_full_ready, 1)
                act.copy(xt_hi[:, b, :], ps_x[b % 2][:, :]).then_inc(xt_hi_ready, 1)

            for b in range(B):
                act.wait_ge(moments_ready, C * (b + 1))
                act.activation(std[:, b * C:(b + 1) * C], moments[:, b * C:(b + 1) * C, 1], ACT.Sqrt,
                               bias=eps[:, 0:1]).then_inc(std_ready, 1)
                if b >= 1:
                    take_transposed(b - 1)
            take_transposed(B - 1)
            act.wait_ge(below_ready, 1)
            act.activation(expd[:, :, :], below[:, :, :], ACT.Exp).then_inc(expd_ready, 1)
            act.wait_ge(angle_ready, 2)
            act.activation(trig[0:N, :], phase[0:N, :], ACT.Sin, scale=-1.0, bias=half_pi[0:N, 0:1]).then_inc(trig_ready, 1)
            act.activation(trig[N:P, :], phase[N:P, :], ACT.Sin).then_inc(trig_ready, 1)

            def take_inside(k):
                act.wait_ge(inside_psum, k + 1)
                if k >= 2:
                    act.wait_ge(inside_moved[k % 2], 16 * (k // 2))
                act.copy(inside[:, k % 2, :, :],
                         ps_side[:, :].rearrange("p (r i) -> p r i", r=4)[:, :, ::-1]).then_inc(inside_ready, 1)

            for s in range(STEPS):
                b, j = divmod(s, BLOCKS)
                act.wait_ge(up_psum, s + 1)
                if s >= 2:
                    act.wait_ge(hidden_ready, s - 1)
                if j < SHARED:
                    act.activation(act_g[:, s % 2, :], ps_g[s % 2][:, :], ACT.Silu).then_inc(act_g_ready, 1)
                else:
                    act.activation(act_g[F:P, s % 2, :], ps_g[s % 2][0:F, :], ACT.Silu).then_inc(act_g_ready, 1)
                if j == 1 and b >= 1:
                    act.wait_ge(down_psum, BLOCKS * b)
                    act.activation(g_all[:, b - 1, :], ps_o[(b - 1) % 2][:, :], ACT.Silu).then_inc(g_ready, 1)
                if side.get(s - 1, ("", 0))[0] == "inside":
                    take_inside(side[s - 1][1])
            act.wait_ge(down_psum, STEPS)
            act.activation(g_all[:, B - 1, :], ps_o[(B - 1) % 2][:, :], ACT.Silu).then_inc(g_ready, 1)

            for b in range(B + 1):
                if b < B:
                    act.wait_ge(gate_psum, b + 1)
                    if b >= 2:
                        act.wait_ge(both_ready, b - 1)
                    act.activation(gated[:, b % 2, :], ps_gate[b % 2][:, :], ACT.Gelu,
                                   bias=gate_b).then_inc(gate_ready, 1)
                if b >= 1:
                    act.wait_ge(ss_psum, b)
                    if b >= 3:
                        act.wait_ge(both_ready, b - 2)
                    act.activation(ssg[:, (b - 1) % 2, :], ps_ss[(b - 1) % 2][:, :], ACT.Gelu,
                                   bias=ss_b).then_inc(ssg_ready, 1)

        @block.vector
        def _(dve):
            done = {}

            def link(ins, s):
                done[s.name] = done.get(s.name, 0) + 1
                ins.then_inc(s, 1)
                dve.wait_ge(s, done[s.name])

            dve.wait_ge(modes_loaded, 16)
            dve.wait_ge(steps_ready, 2)
            link(dve.tensor_scalar(omega[:, :], freq, TWO_PI, None, ALU.mult), mode)
            dve.wait_ge(decay_exp_ready, 1)
            dve.tensor_scalar(rate[:, :], rate[:, :], -1.0, None, ALU.mult).then_inc(rate_ready, 1)
            link(dve.tensor_scalar(phase[:, :], steps[:, :], omega[:, 0:1], None, ALU.mult), mode)
            link(dve.tensor_scalar(turns[:, :], phase[:, :], 1.0 / TWO_PI, ROUND, ALU.mult, ALU.add), mode)
            link(dve.tensor_scalar(turns[:, :], turns[:, :], ROUND, None, ALU.subtract), mode)
            for tp in (TP1, TP2, TP3):
                link(dve.scalar_tensor_tensor(phase[:, :], turns[:, :], -tp, phase[:, :], ALU.mult, ALU.add), mode)
            link(dve.tensor_scalar(phase[:, :], phase[:, :], PI_BELOW, -PI_BELOW, ALU.min, ALU.max), mode)
            dve.scalar_tensor_tensor(turns[0:N, :], phase[0:N, :], -1.0, phase[0:N, :], ALU.mult,
                                     ALU.max).then_inc(angle_ready, 1)
            dve.wait_ge(angle_ready, 1)
            dve.tensor_copy(phase[0:N, :], turns[0:N, :]).then_inc(angle_ready, 1)
            dve.tensor_tensor(mix[:, :], part(modes_sb, MODE_COLS, "in"), part(modes_sb, MODE_COLS, "out"),
                              ALU.mult).then_inc(mix_ready, 1)
            dve.wait_ge(mix_ready, 1)
            dve.tensor_scalar(mix_signed[:, :], mix[:, :], sign, None, ALU.mult).then_inc(mix_ready, 1)

            def statistics(b):
                dve.wait_ge(x_loaded[b], 16)
                for c in range(C):
                    dve.bn_stats(stats[:, b * C + c, :], x_tok[:, b, c, :]).then_inc(stats_ready, 1)
                dve.wait_ge(stats_ready, C * (b + 1))
                for c in range(C):
                    dve.bn_aggr(moments[:, b * C + c, :], stats[:, b * C + c, :]).then_inc(moments_ready, 1)

            def normalise(b):
                dve.wait_ge(std_ready, b + 1)
                dve.reciprocal(rstd[:, b * C:(b + 1) * C], std[:, b * C:(b + 1) * C]).then_inc(rstd_ready, 1)
                dve.wait_ge(rstd_ready, b + 1)
                dve.wait_ge(moments_ready, C * (b + 1))
                for c in range(C):
                    t = b * C + c
                    dve.tensor_scalar(xn[:, b, c, :], x_tok[:, b, c, :], moments[:, t, 0:1], rstd[:, t:t + 1],
                                      ALU.subtract, ALU.mult).then_inc(xn_ready, 1)

            for b in range(B):
                statistics(b)
                if b >= 1:
                    normalise(b - 1)
            normalise(B - 1)

            def over_experts(t):
                return t[:, :].unsqueeze(2).to_broadcast([P, NT, E])

            logits = ps_logit[:, 0:NT * E].rearrange("p (t e) -> p t e", e=E)
            dve.wait_ge(rank_ready, 1)
            link(dve.tensor_copy(rank[:, :, :], ranki[:, :, :]), route)
            dve.wait_ge(logits_psum, B)
            link(dve.tensor_reduce(top[:, :], logits, AX, ALU.max), route)
            dve.tensor_tensor(below[:, :, :], logits, over_experts(top), ALU.subtract).then_inc(below_ready, 1)
            dve.wait_ge(below_ready, 1)
            link(dve.scalar_tensor_tensor(key[:, :, :], below[:, :, :], 0.0, rank[:, :, :], ALU.is_ge, ALU.mult), route)
            link(dve.tensor_reduce(best[:, :], key[:, :, :], AX, ALU.max), route)
            link(dve.tensor_tensor(first[:, :, :], key[:, :, :], over_experts(best), ALU.is_equal), route)
            link(dve.scalar_tensor_tensor(rest[:, :, :], first[:, :, :], -BIG, below[:, :, :], ALU.mult, ALU.add), route)
            link(dve.tensor_reduce(top[:, :], rest[:, :, :], AX, ALU.max), route)
            link(dve.tensor_tensor(rest[:, :, :], rest[:, :, :], over_experts(top), ALU.is_ge), route)
            link(dve.tensor_tensor(key[:, :, :], rest[:, :, :], rank[:, :, :], ALU.mult), route)
            link(dve.tensor_reduce(best[:, :], key[:, :, :], AX, ALU.max), route)
            link(dve.tensor_tensor(second[:, :, :], key[:, :, :], over_experts(best), ALU.is_equal), route)
            link(dve.tensor_tensor(first[:, :, :], first[:, :, :], second[:, :, :], ALU.add), route)
            dve.wait_ge(expd_ready, 1)
            link(dve.tensor_reduce(total[:, :], expd[:, :, :], AX, ALU.add), route)
            link(dve.reciprocal(rtotal[:, :], total[:, :]), route)
            link(dve.tensor_tensor(weight[:, :, :], expd[:, :, :], first[:, :, :], ALU.mult), route)
            link(dve.tensor_tensor(weight[:, :, :], weight[:, :, :], over_experts(rtotal), ALU.mult), route)
            link(dve.tensor_copy(parts[:, :, 0, :], weight[:, :, :]), route)
            link(dve.tensor_tensor(remain[:, :, :], weight[:, :, :], parts[:, :, 0, :], ALU.subtract), route)
            link(dve.tensor_copy(parts[:, :, 1, :], remain[:, :, :]), route)
            link(dve.tensor_tensor(remain[:, :, :], remain[:, :, :], parts[:, :, 1, :], ALU.subtract), route)
            dve.tensor_copy(parts[:, :, 2, :], remain[:, :, :]).then_inc(parts_ready, 1)
            dve.wait_ge(weight_psum, 1)
            dve.tensor_copy(weight_t[:, :, :].rearrange("p b j -> p (b j)"), ps_w16).then_inc(weight_t_ready, 1)

            dve.wait_ge(trig_ready, 2)
            dve.wait_ge(amp_ready, 1)
            dve.tensor_tensor(table[:, :], amp[:, :], trig[:, :], ALU.mult).then_inc(table_ready, 1)

            for s in range(STEPS):
                b, j = divmod(s, BLOCKS)
                buf = s % 2
                dve.wait_ge(act_g_ready, s + 1)
                dve.wait_ge(up_psum, s + 1)
                if s >= 2:
                    dve.wait_ge(down_psum, s - 1)
                if j < SHARED:
                    dve.tensor_tensor(prod[:, buf, :], act_g[:, buf, :], ps_u[buf][:, :],
                                      ALU.mult).then_inc(prod_ready, 1)
                    dve.wait_ge(prod_ready, routed_steps(s) + 1)
                    dve.wait_ge(bcast_psum, routed_steps(s) + 1)
                    dve.tensor_tensor(hidden[:, buf, :], prod[:, buf, :], ps_w[:, :],
                                      ALU.mult).then_inc(hidden_ready, 1)
                else:
                    dve.tensor_tensor(hidden[F:P, buf, :], act_g[F:P, buf, :], ps_g[buf][F:P, :],
                                      ALU.mult).then_inc(hidden_ready, 1)
                kind, i = side.get(s - 1, ("", 0))
                if kind == "taps":
                    dve.wait_ge(taps_psum, 1)
                    dve.wait_ge(kpad_ready, 1)
                    dve.tensor_copy(kpad[:, 0:P], ps_side[:, 0:P]).then_inc(kpad_ready, 1)
                    dve.tensor_copy(decay_t[:, :, :].rearrange("p k m -> p (k m)"),
                                    ps_side[:, P:L]).then_inc(decay_t_ready, 1)
                if kind == "state":
                    c, half = STATES[i]
                    dve.wait_ge(mix_ready, 2)
                    dve.wait_ge(state_psum, i + 1)
                    dve.tensor_tensor(state[:, c - 1, 4 * half:4 * half + 4, :],
                                      ps_side[:, :].rearrange("m (b h) -> m b h", h=H),
                                      mix_signed[:, :].unsqueeze(1).to_broadcast([P, 4, H]),
                                      ALU.mult).then_inc(state_ready, 1)

            for b in range(B + 2):
                if b < B:
                    dve.wait_ge(inter_psum, b + 1)
                    dve.wait_ge(conv_loaded[b], 16)
                    later = conv[:, b, 1:C, :].rearrange("p c i -> p (c i)")
                    dve.tensor_tensor(later, later, ps_inter[b % 2][:, P:L], ALU.add).then_inc(conv_ready, 1)
                if 1 <= b <= B:
                    k = b - 1
                    dve.wait_ge(gate_ready, k + 1)
                    dve.wait_ge(ssg_ready, k + 1)
                    if k >= 2:
                        dve.wait_ge(fin_psum, k - 1)
                    dve.tensor_tensor(both[:, k % 2, :], gated[:, k % 2, :], ssg[:, k % 2, :],
                                      ALU.mult).then_inc(both_ready, 1)
                if b >= 2:
                    k = b - 2
                    dve.wait_ge(late_loaded, 32)
                    dve.wait_ge(fin_psum, k + 1)
                    dve.tensor_tensor(s_sum[:, k % 2, :].rearrange("p (c h) -> p c h", h=H),
                                      ps_fin[k % 2][:, :].rearrange("p (c h) -> p c h", h=H),
                                      fin_b_sb[:, :].unsqueeze(1).to_broadcast([P, C, H]),
                                      ALU.add).then_inc(s_sum_ready, 1)
                    dve.wait_ge(s_sum_ready, k + 1)
                    dve.wait_ge(g_ready, k + 1)
                    if k >= 2:
                        dve.wait_ge(y_ready, k - 1)
                    dve.tensor_tensor(s_g[:, k % 2, :], s_sum[:, k % 2, :], g_all[:, k, :],
                                      ALU.mult).then_inc(s_g_ready, 1)

        @block.tensor
        def _(pe):
            def three(ps, hi, lo, b):
                pe.matmul(ps, hi, xt_hi[:, b, :], start=True, stop=False)
                pe.matmul(ps, lo, xt_hi[:, b, :], start=False, stop=False)
                return pe.matmul(ps, hi, xt_lo[:, b, :], start=False, stop=True)

            def turn_tokens(b):
                pe.wait_ge(xn_ready, C * (b + 1))
                if b >= 2:
                    pe.wait_ge(xt_hi_ready, b - 1)
                for c in range(C):
                    mm = pe.transpose(ps_x[b % 2][:, c * P:(c + 1) * P], xn[:, b, c, :], ident)
                mm.then_inc(xt_psum, 1)

            def route_tokens(b):
                pe.wait_ge(xt_full_ready, b + 1)
                for c in range(C):
                    t = b * C + c
                    mm = pe.matmul(ps_logit[:, t * E:(t + 1) * E], xt_full[:, b % 2, c * P:(c + 1) * P], router,
                                   start=True, stop=True)
                mm.then_inc(logits_psum, 1)

            pe.wait_ge(early_loaded, 16)
            for b in range(B):
                turn_tokens(b)
                if b >= 1:
                    route_tokens(b - 1)
            route_tokens(B - 1)

            def up(s):
                b, j = divmod(s, BLOCKS)
                if s == 0:
                    pe.wait_ge(wide_lo_ready, 1)
                    pe.wait_ge(xt_hi_ready, B)
                pe.wait_ge(xt_lo_ready, b + 1)
                if s >= 2:
                    pe.wait_ge(hidden_ready, s - 1)
                mm = three(ps_g[s % 2][:, :], gu(wide_hi, 2 * j), gu(wide_lo, 2 * j), b)
                if j < SHARED:
                    if s == 0:
                        pe.wait_ge(below_ready, 1)
                    mm = three(ps_u[s % 2][:, :], gu(wide_hi, 2 * j + 1), gu(wide_lo, 2 * j + 1), b)
                mm.then_inc(up_psum, 1)

            def spread_weights(s):
                b, j = divmod(s, BLOCKS)
                if j == SHARED:
                    return
                if s == 0:
                    pe.wait_ge(select_loaded, 32)
                    pe.wait_ge(parts_ready, 2)
                    for i in range(B):
                        mm = pe.transpose(ps_w16[:, i * P:(i + 1) * P],
                                          parts[:, i * C:(i + 1) * C, :, :].rearrange("p t k e -> p (t k e)"),
                                          ident16[:, :])
                    mm.then_inc(weight_psum, 1)
                    pe.wait_ge(weight_t_ready, 1)
                else:
                    pe.wait_ge(hidden_ready, s if j else s - 1)
                for c in range(C):
                    mm = pe.matmul(ps_w[:, c * P:(c + 1) * P], select_sb[:, j, c, :], weight_t[:, b, :],
                                   start=True, stop=True)
                mm.then_inc(bcast_psum, 1)

            def down(s):
                b, j = divmod(s, BLOCKS)
                if s == 0:
                    pe.wait_ge(late_loaded, 32)
                pe.wait_ge(hidden_ready, s + 1)
                if j == 0 and b >= 2:
                    pe.wait_ge(g_ready, b - 1)
                lo = F if j == SHARED else 0
                for c in range(C):
                    mm = pe.matmul(ps_o[b % 2][:, c * P:(c + 1) * P], hidden[lo:P, s % 2, c * P:(c + 1) * P],
                                   wd[lo:P, j, :], start=(j == 0 and c == 0), stop=(j == SHARED),
                                   skip_group_check=True)
                mm.then_inc(down_psum, 1)

            def taps():
                pe.wait_ge(table_ready, 1)
                pe.wait_ge(mix_ready, 1)
                pe.matmul(ps_side[:, 0:P], mix[0:N, :], table[0:N, TAB - P:TAB], start=True, stop=True)
                for k in range(C - 1):
                    at = FWD + (C - 2 - k) * P
                    mm = pe.transpose(ps_side[:, (k + 1) * P:(k + 2) * P], table[:, at:at + P], ident)
                mm.then_inc(taps_psum, 1)

            def inside_chunks(k):
                pe.wait_ge(toeplitz_loaded[k % RING], 16 * (k // RING + 1))
                for r in range(4):
                    for q in range(4):
                        u = xn[:, :, :, k * CH + 4 * r + q].rearrange("j b c -> j (b c)")
                        mm = pe.matmul(ps_side[32 * q:32 * q + 32, r * P:(r + 1) * P], u,
                                       toeplitz[:, k % RING, 4 * r + q, :], start=True, stop=True,
                                       skip_group_check=True)
                mm.then_inc(inside_psum, 1)

            def chunk_state(i):
                c, half = STATES[i]
                for before in range(c):
                    mm = pe.matmul(ps_side[:, :], decay_t[:, c - 1 - before, :],
                                   xn[:, 4 * half:4 * half + 4, before, :], start=(before == 0),
                                   stop=(before == c - 1))
                mm.then_inc(state_psum, 1)

            for s in range(STEPS + 1):
                if s < STEPS:
                    up(s)
                if s >= 1:
                    down(s - 1)
                if s < STEPS:
                    spread_weights(s)
                if s in side:
                    side_free(pe, s)
                    kind, i = side[s]
                    {"taps": lambda i: taps(), "inside": inside_chunks, "state": chunk_state}[kind](i)

            def gate(b):
                if b < 2:
                    pe.wait_ge(hidden_ready, STEPS)
                else:
                    pe.wait_ge(gate_ready, b - 1)
                three(ps_gate[b % 2][:, :], wide_hi[:, gate_at:gate_at + H], wide_lo[:, gate_at:gate_at + H],
                      b).then_inc(gate_psum, 1)

            def inter(b):
                if b == 0:
                    pe.wait_ge(state_ready, len(STATES))
                if b >= 2:
                    pe.wait_ge(conv_ready, b - 1)
                for c in range(1, C):
                    mm = pe.matmul(ps_inter[b % 2][:, c * P:(c + 1) * P], state[:, c - 1, b, :],
                                   table[:, 1:1 + P], start=True, stop=True)
                mm.then_inc(inter_psum, 1)

            def ss(b):
                pe.wait_ge(conv_ready, b + 1)
                if b == 0:
                    pe.wait_ge(hidden_ready, STEPS)
                if b == 1:
                    pe.wait_ge(inside_ready, B)
                if b >= 2:
                    pe.wait_ge(ssg_ready, b - 1)
                pe.matmul(ps_ss[b % 2][:, :], ss_w, conv[:, b, :, :].rearrange("p c i -> p (c i)"),
                          start=True, stop=True).then_inc(ss_psum, 1)

            def fin(b):
                pe.wait_ge(both_ready, b + 1)
                if b < 2:
                    pe.wait_ge(g_ready, B)
                else:
                    pe.wait_ge(s_sum_ready, b - 1)
                for c in range(C):
                    mm = pe.matmul(ps_fin[b % 2][:, c * P:(c + 1) * P], both[:, b % 2, c * P:(c + 1) * P], fin_w,
                                   start=True, stop=True)
                mm.then_inc(fin_psum, 1)

            for b in range(B + 2):
                if b < B:
                    gate(b)
                    inter(b)
                if 1 <= b <= B:
                    ss(b - 1)
                if b >= 2:
                    fin(b - 2)


def kernel(**inputs):
    import concourse.bacc as bacc
    from concourse.bass_utils import run_bass_kernel_spmd as run

    a = {name: np.asarray(v) for name, v in inputs.items()}
    f32 = np.float32

    def col(v):
        return v.reshape(-1, 1)

    def twice(v):
        return np.concatenate([v, v], axis=0)

    sign = np.concatenate([np.ones((N, 1), f32), -np.ones((N, 1), f32)])
    modes = np.concatenate([
        col(twice(a["L0_attn_frequencies"])), col(twice(a["L0_attn_decays"])), sign,
        twice(a["L0_attn_in_proj"].T), twice(a["L0_attn_out_proj"])], axis=1)
    early = np.concatenate([np.eye(P, dtype=f32), a["L0_ffn_gate_w"].T], axis=1)
    wg, wu = a["L0_ffn_wg"], a["L0_ffn_wu"]
    gus = []
    for j in range(PAIRS):
        for w in (wg, wu):
            gus.append(w[2 * j:2 * j + 2].reshape(P, H).T)
    gus.append(np.concatenate([a["L0_ffn_sg"], a["L0_ffn_su"]], axis=0).T)
    wide = np.concatenate(gus + [a["L0_attn_gate_W"].T], axis=1)
    downs = [a["L0_ffn_wd"][2 * j:2 * j + 2].transpose(0, 2, 1).reshape(P, H) for j in range(PAIRS)]
    downs.append(twice(a["L0_ffn_sd"].T))
    late = np.concatenate(downs + [a["L0_attn_ss_W"].T, a["L0_attn_fin_W"].T, col(a["L0_attn_ss_b"]),
                                   col(a["L0_attn_gate_b"])], axis=1)
    import ml_dtypes
    bf = ml_dtypes.bfloat16
    select = np.zeros((C, 4, E, PAIRS, C, 2, F), bf)
    for c in range(C):
        for e in range(E):
            select[c, 0:3, e, e // 2, c, e % 2, :] = 1
    arrays = {
        "x": a["L0_attn_x"], "modes": modes, "early": early, "wide": wide, "late": late,
        "fin_b": a["L0_attn_fin_b"], "ident_bf": np.eye(P, dtype=bf), "select": select.reshape(P, PAIRS, C, P),
    }
    arrays = {k: np.ascontiguousarray(v) for k, v in arrays.items()}
    nc = bacc.Bacc("TRN2", target_bir_lowering=False, num_devices=1)
    args = [nc.dram_tensor(k, v.shape, mybir.dt.from_np(v.dtype), kind="ExternalInput").ap()
            for k, v in arrays.items()]
    out = nc.dram_tensor("out", (B, L, H), F32, kind="ExternalOutput").ap()
    layer(nc, *args, out)
    r = run(nc, [arrays], core_ids=[0])
    return r.results[0]["out"]
```

```python
from contextlib import ExitStack

import numpy as np

import concourse.bass as bass
from concourse import mybir

F32 = mybir.dt.float32
F32R = mybir.dt.float32r
BF16 = mybir.dt.bfloat16
I32 = mybir.dt.int32
ALU = mybir.AluOpType
ACT = mybir.ActivationFunctionType
AX = mybir.AxisListType.X

P = 128
B, L, H = 8, 512, 128
C = L // P
NT = B * C
N = 64
E, F = 8, 64
EPS = 1e-5
PAIRS = E // 2
BLOCKS = PAIRS + 1
SHARED = PAIRS
GU = 2 * PAIRS + 1
RING = 2
CH = 16

def columns(*parts):
    at, out = 0, {}
    for name, width in parts:
        out[name] = (at, width)
        at += width
    return out, at


MODE_COLS, MODE_W = columns(("freq", 1), ("decay", 1), ("sign", 1), ("in", H), ("out", H))
EARLY_COLS, EARLY_W = columns(("ident", P), ("router", E))
WIDE_COLS, WIDE_W = columns(("gu", GU * P), ("gate", H), ("fin", H), ("wd", BLOCKS * H))
LATE_COLS, LATE_W = columns(("ss", H), ("fin", H), ("ss_b", 1), ("gate_b", 1), ("fin_b", 1))

TWO_PI = 6.283185307179586
TP1 = 6.25
TP2 = 17.0 / 512.0
TP3 = TWO_PI - TP1 - TP2
ROUND = 1.5 * 2.0 ** 23
PI_BELOW = 3.1415925
BIG = 3.0e38

FWD = P + 1
REV = P
TAB = FWD + REV


def layer(nc, x, modes, early, wide, late, ident_bf, select, out):
    ctx = ExitStack()
    with ctx:
        def sb(name, shape, dt=F32):
            return ctx.enter_context(nc.sbuf_tensor(name, shape, dt))

        def sem(name):
            return ctx.enter_context(nc.semaphore(name))

        x_tok = sb("x_tok", [P, B, C, H])
        modes_sb = sb("modes_sb", [P, MODE_W])
        early_sb = sb("early_sb", [P, EARLY_W])
        state = sb("state", [P, C - 1, B, H])
        wide_sb = state[:, :, :, :].rearrange("p c b h -> p (c b h)")[:, 0:WIDE_W]
        late_sb = sb("late_sb", [P, LATE_W])
        ident16 = sb("ident16", [P, P], BF16)
        select_sb = sb("select_sb", [P, PAIRS, C, P], BF16)
        wide_hi = sb("wide_hi", [P, WIDE_W], F32R)
        wide_lo = sb("wide_lo", [P, WIDE_W], F32R)

        def part(t, cols, name):
            at, width = cols[name]
            return t[:, at:at + width]

        freq = part(modes_sb, MODE_COLS, "freq")
        decay = part(modes_sb, MODE_COLS, "decay")
        sign = part(modes_sb, MODE_COLS, "sign")
        ident = part(early_sb, EARLY_COLS, "ident")
        router = part(early_sb, EARLY_COLS, "router")
        wd_at = WIDE_COLS["wd"][0]
        ss_w = part(late_sb, LATE_COLS, "ss")
        fin_w = part(late_sb, LATE_COLS, "fin")
        ss_b = part(late_sb, LATE_COLS, "ss_b")
        gate_b = part(late_sb, LATE_COLS, "gate_b")
        fin_b = part(late_sb, LATE_COLS, "fin_b")

        def gu(t, block):
            return t[:, block * P:(block + 1) * P]

        gate_at, fin_at = WIDE_COLS["gate"][0], WIDE_COLS["fin"][0]
        PIECES = [slice(0, 2 * P), slice(2 * P, 4 * P), slice(4 * P, GU * P), slice(GU * P, WIDE_W)]

        stats = sb("stats", [P, NT, 6])
        moments = sb("moments", [P, NT, 2])
        half_pi = sb("half_pi", [P, 1])
        minus_half = sb("minus_half", [P, C])
        spread = sb("spread", [P, NT])
        rstd = sb("rstd", [P, NT])
        xn = sb("xn", [P, B, C, H])
        xt_full = sb("xt_full", [P, 2, L])
        xt_hi = sb("xt_hi", [P, B, L], F32R)
        xt_lo = sb("xt_lo", [P, B, L], F32R)

        rank = sb("rank", [P, NT, E])
        ranki = sb("ranki", [P, NT, E], I32)
        logits = sb("logits", [P, NT, E])
        top = sb("top", [P, NT])
        below = sb("below", [P, NT, E])
        expd = sb("expd", [P, NT, E])
        total = sb("total", [P, NT])
        rtotal = sb("rtotal", [P, NT])
        key = sb("key", [P, NT, E])
        best = sb("best", [P, NT])
        first = sb("first", [P, NT, E])
        rest = sb("rest", [P, NT, E])
        second = sb("second", [P, NT, E])
        weight = sb("weight", [P, NT, E])
        remain = sb("remain", [P, NT, E])
        parts = sb("parts", [P, NT, 4, E], BF16)
        weight_t = sb("weight_t", [P, B, P], BF16)

        omega = sb("omega", [P, 1])
        rate = sb("rate", [P, 1])
        steps = sb("steps", [P, TAB], I32)
        phase = sb("phase", [P, TAB])
        amp = sb("amp", [P, TAB])
        trig = sb("trig", [P, TAB])
        turns = trig
        table = sb("table", [P, TAB])
        mix = sb("mix", [P, H])
        mix_signed = sb("mix_signed", [P, H])
        decay_t = sb("decay_t", [P, P])
        turn_real = sb("turn_real", [P, 1])
        turn_imag = sb("turn_imag", [P, 1])
        swapped = sb("swapped", [P, B // 2, H])
        kpad = sb("kpad", [P, 2 * P])
        toeplitz = sb("toeplitz", [P, RING, CH, P])
        inside = sb("inside", [P, 2, 4, P])
        conv = xn

        act_g = sb("act_g", [P, 2, L])
        hidden = sb("hidden", [P, BLOCKS, L])
        hidden_hi = sb("hidden_hi", [P, 3, L], F32R)
        hidden_lo = sb("hidden_lo", [P, 3, L], F32R)
        scaled = sb("scaled", [P, 2, L])
        g_all = sb("g_all", [P, B, L])
        gated, ssg, both = act_g, hidden[:, 0:2, :], hidden[:, 2:4, :]
        both_hi, both_lo = hidden_hi, hidden_lo
        y_out = toeplitz[:, 0, 0:8, :].rearrange("p (n r) i -> p n (r i)", n=2)

        k_dram = nc.dram_tensor("k_dram", (P, 2 * P), F32, kind="Internal").ap()

        conv_dram = nc.dram_tensor("conv_dram", (H, NT, P), F32, kind="Internal").ap()

        def bank(name):
            return ctx.enter_context(nc.psum_tensor(name, [P, L], F32))

        ps_g = [bank("ps_g0"), bank("ps_g1")]
        ps_u = [bank("ps_u0"), bank("ps_u1")]
        ps_w = [bank("ps_w0"), bank("ps_w1")]
        ps_side = bank("ps_side")
        ps_o = bank("ps_o")
        ps_gate, ps_inter, ps_ss, ps_fin = ps_g, ps_u, ps_w, ps_o
        ps_side16 = ps_side[:, :].bitcast(BF16)

        x_loaded = [sem(f"x_loaded{b}") for b in range(B)]
        modes_loaded, early_loaded = sem("modes_loaded"), sem("early_loaded")
        late_loaded = sem("late_loaded")
        wide_loaded = [sem(f"wide_loaded{i}") for i in range(4)]
        select_loaded = sem("select_loaded")
        consts_ready, steps_ready, rank_ready = sem("consts_ready"), sem("steps_ready"), sem("rank_ready")
        stats_ready, moments_ready, spread_ready = sem("stats_ready"), sem("moments_ready"), sem("spread_ready")
        rstd_ready, xn_ready = sem("rstd_ready"), sem("xn_ready")
        xt_psum, xt_full_ready, xt_hi_ready, xt_lo_ready = (
            sem("xt_psum"), sem("xt_full_ready"), sem("xt_hi_ready"), sem("xt_lo_ready"))
        wide_hi_ready, wide_lo_ready = sem("wide_hi_ready"), sem("wide_lo_ready")
        logits_psum, below_ready, expd_ready = sem("logits_psum"), sem("below_ready"), sem("expd_ready")
        route, mode, parts_cleared = sem("route"), sem("mode"), sem("parts_cleared")
        shared_cleared = sem("shared_cleared")
        parts_ready, weight_psum, weight_t_ready = sem("parts_ready"), sem("weight_psum"), sem("weight_t_ready")
        rate_ready, amp_ready, angle_ready, trig_ready = (
            sem("rate_ready"), sem("amp_ready"), sem("angle_ready"), sem("trig_ready"))
        decay_exp_ready = sem("decay_exp_ready")
        mix_ready, table_ready, taps_psum = sem("mix_ready"), sem("table_ready"), sem("taps_psum")
        kpad_ready, decay_t_ready, k_stored = sem("kpad_ready"), sem("decay_t_ready"), sem("k_stored")
        toeplitz_loaded = [sem(f"toeplitz_loaded{i}") for i in range(RING)]
        up_psum, act_g_ready, prod_ready = sem("up_psum"), sem("act_g_ready"), sem("prod_ready")
        bcast_psum, hidden_ready, down_psum = sem("bcast_psum"), sem("hidden_ready"), sem("down_psum")
        g_ready = sem("g_ready")
        hidden_hi_ready, hidden_lo_ready = sem("hidden_hi_ready"), sem("hidden_lo_ready")
        both_hi_ready, both_lo_ready = sem("both_hi_ready"), sem("both_lo_ready")
        inside_psum, inside_ready = sem("inside_psum"), sem("inside_ready")
        conv_loaded = [sem(f"conv_loaded{b}") for b in range(B)]
        inside_moved = [sem(f"inside_moved{i}") for i in range(2)]
        state_psum, state_taken, state_ready = sem("state_psum"), sem("state_taken"), sem("state_ready")
        swapped_ready, turn_ready, chain = sem("swapped_ready"), sem("turn_ready"), sem("chain")
        gate_psum, gate_ready, inter_psum, conv_ready = (
            sem("gate_psum"), sem("gate_ready"), sem("inter_psum"), sem("conv_ready"))
        ss_psum, ssg_ready, both_ready = sem("ss_psum"), sem("ssg_ready"), sem("both_ready")
        fin_psum, scaled_ready, turned_psum, y_ready = (
            sem("fin_psum"), sem("scaled_ready"), sem("turned_psum"), sem("y_ready"))
        logits_taken = sem("logits_taken")
        y_stored = [sem(f"y_stored{i}") for i in range(2)]

        STEPS = B * BLOCKS

        def routed_steps(s):
            return s // BLOCKS * PAIRS + min(s % BLOCKS, PAIRS)

        STATES = [(c, half) for half in range(2) for c in range(1, C)]
        FIRST_JOBS = [("turn", 0), ("route", 0)]
        JOBS_AT = {
            0: [None, ("turn", 1)], 1: [("route", 1), ("weights", 0)], 2: [None, ("turn", 2)],
            3: [None, ("route", 2)], 7: [("weights", 1)], 9: [None, ("turn", 3)], 10: [("route", 3)],
            11: [None, ("turn", 4)], 12: [("route", 4)], 16: [None, ("weights", 2)], 17: [None, ("taps", 0)],
            18: [None, ("turn", 5)], 19: [None, ("route", 5)], 20: [("state", 0), ("turn", 6)],
            21: [None, ("route", 6)], 22: [("state", 1), ("turn", 7)], 23: [("route", 7)],
            24: [("state", 2), ("inside", 0)], 26: [("inside", 1), ("weights", 3)],
            27: [("inside", 2), ("state", 3)], 30: [None, ("inside", 3)], 31: [("state", 4)],
            32: [("inside", 4), ("state", 5)], 34: [("inside", 5)], 37: [("inside", 6), ("inside", 7)],
        }
        LAST_JOB = ("result", 0)
        ALL_JOBS = FIRST_JOBS + [job for s in sorted(JOBS_AT) for job in JOBS_AT[s] if job] + [LAST_JOB]

        def job_at(s, place):
            jobs = JOBS_AT.get(s, [])
            return (jobs[place] if place < len(jobs) else None) or ("", 0)

        GROUPS = [(0, 1), (1, 2), (3, 2), (5, 3)]
        VECTOR_AT = {
            0: [("statistics", 2)], 1: [("normalise", 2)], 3: [("below", 1), ("pick", 1)],
            4: [("pick_second", 1), ("modes", 0)], 5: [("weigh", 1), ("split", 1)], 7: [("statistics", 3)],
            8: [("normalise", 3)], 9: [("statistics", 4)], 10: [("normalise", 4)], 11: [("modes", 1)],
            12: [("below", 2), ("pick", 2)], 13: [("pick_second", 2), ("weigh", 2)], 14: [("modes", 2)],
            15: [("split", 2), ("modes", 3)], 16: [("statistics", 5)],
            17: [("normalise", 5), ("statistics", 6)], 19: [("normalise", 6)], 20: [("statistics", 7)],
            21: [("normalise", 7)], 23: [("below", 3)],
            24: [("pick", 3), ("pick_second", 3), ("weigh", 3), ("split", 3)],
        }

        def steps_of(kind):
            return {s: i for s, work in VECTOR_AT.items() for k, i in work if k == kind}

        STATISTICS_AT, BELOW_AT, MODES_AT = steps_of("statistics"), steps_of("below"), steps_of("modes")
        SPREAD_LAG, SPLIT_LAG = 2, 3
        LAG = 5
        G_AT = {b * BLOCKS + SHARED + LAG + 1: b for b in range(B)}

        def followed(i):
            return sum(c > 1 for c, half in STATES[:i + 1])

        def bank_free(eng, job):
            n = ALL_JOBS.index(job)
            if n == 0:
                return
            kind, i = ALL_JOBS[n - 1]
            if kind == "turn":
                eng.wait_ge(xt_hi_ready, i + 1)
            elif kind == "route":
                eng.wait_ge(logits_taken, i + 1)
            elif kind == "weights":
                eng.wait_ge(weight_t_ready, i + 1)
            elif kind == "taps":
                eng.wait_ge(kpad_ready, 2)
                eng.wait_ge(decay_t_ready, 1)
            elif kind == "inside":
                eng.wait_ge(inside_ready, i + 1)
            else:
                eng.wait_ge(state_taken, i + 1)

        block = ctx.enter_context(nc.Block())

        @block.sync
        def _(sp):
            for b in range(B):
                sp.dma_start(x_tok[:, b], x[b].rearrange("(c j) h -> j c h", j=P)).then_inc(x_loaded[b], 16)
                if b == 0:
                    sp.dma_start(early_sb[:, :], early).then_inc(early_loaded, 16)
                if b == 1:
                    sp.dma_start(wide_sb[:, PIECES[0]], wide[:, PIECES[0]]).then_inc(wide_loaded[0], 16)
                    sp.dma_start(modes_sb[:, :], modes).then_inc(modes_loaded, 16)
                    for piece in (1, 2, 3):
                        sp.dma_start(wide_sb[:, PIECES[piece]], wide[:, PIECES[piece]]).then_inc(
                            wide_loaded[piece], 16)
                    sp.dma_start(ident16[:, :], ident_bf).then_inc(select_loaded, 16)
                    sp.dma_start(select_sb[:, :, :, :], select).then_inc(select_loaded, 16)
                    sp.dma_start(late_sb[:, :], late).then_inc(late_loaded, 16)
            sp.wait_ge(kpad_ready, 2)
            sp.dma_start(k_dram, kpad[:, :]).then_inc(k_stored, 16)
            sp.wait_ge(k_stored, 16)

            def load_toeplitz(k):
                if k >= RING:
                    sp.wait_ge(inside_psum, k - RING + 1)
                src = bass.AP(k_dram.tensor, k_dram.offset + k * CH * 2 * P, [[1, P], [2 * P, CH], [1, P]])
                sp.dma_start(toeplitz[:, k % RING], src).then_inc(toeplitz_loaded[k % RING], 16)

            for k in range(RING):
                load_toeplitz(k)
            for k in range(B):
                sp.wait_ge(inside_ready, k + 1)
                sp.dma_start(conv_dram[k * CH:(k + 1) * CH].rearrange("(r q) m i -> (q m) r i", q=4),
                             inside[:, k % 2, :, :]).then_inc(inside_moved[k % 2], 16)
                if k + RING < B:
                    load_toeplitz(k + RING)
            for i in range(2):
                sp.wait_ge(inside_moved[i], 16 * (B // 2))
            for b in range(B):
                sp.dma_start(conv[:, b, :, :], conv_dram[:, b * C:(b + 1) * C, :]).then_inc(conv_loaded[b], 16)
            for b in range(B):
                sp.wait_ge(y_ready, b + 1)
                sp.dma_start(out[b].rearrange("(c j) h -> j c h", j=P),
                             y_out[:, b % 2, :].rearrange("j (c h) -> j c h", c=C)).then_inc(y_stored[b % 2], 16)
            for i in range(2):
                sp.wait_ge(y_stored[i], 16 * (B // 2))

        @block.gpsimd
        def _(pool):
            pool.memset(minus_half[:, :], -0.5).then_inc(consts_ready, 1)
            pool.memset(half_pi[:, :], TWO_PI / 4).then_inc(consts_ready, 1)
            pool.iota(ranki[:, :, :], [[0, NT], [-1, E]], base=E, channel_multiplier=0).then_inc(rank_ready, 1)
            pool.iota(steps[:, 0:FWD], [[1, FWD]], base=0, channel_multiplier=0).then_inc(steps_ready, 1)
            pool.iota(steps[:, FWD:TAB], [[-1, REV]], base=REV - 1, channel_multiplier=0).then_inc(steps_ready, 1)
            pool.wait_ge(consts_ready, 1)

            def root(b):
                pool.wait_ge(spread_ready, b + 1)
                at = slice(b * C, (b + 1) * C)
                pool.tensor_tensor(rstd[:, at], spread[:, at], minus_half[:, :], ALU.pow).then_inc(rstd_ready, 1)

            def low_part(b):
                pool.wait_ge(xt_full_ready, b + 1)
                pool.wait_ge(xt_hi_ready, b + 1)
                pool.tensor_tensor(xt_lo[:, b, :], xt_full[:, b % 2, :], xt_hi[:, b, :].bitcast(F32),
                                   ALU.subtract).then_inc(xt_lo_ready, 1)

            def wide_low_part(n):
                at = PIECES[n]
                pool.wait_ge(wide_hi_ready, n + 1)
                pool.wait_ge(wide_loaded[n], 16)
                pool.tensor_tensor(wide_lo[:, at], wide_sb[:, at], wide_hi[:, at].bitcast(F32),
                                   ALU.subtract).then_inc(wide_lo_ready, 1)

            def hidden_low_part(s):
                pool.wait_ge(hidden_hi_ready, s + 1)
                if s == SHARED:
                    pool.wait_ge(shared_cleared, 1)
                if s >= 3:
                    pool.wait_ge(down_psum, s - 2)
                pool.tensor_tensor(hidden_lo[:, s % 3, :], hidden[:, s % BLOCKS, :],
                                   hidden_hi[:, s % 3, :].bitcast(F32), ALU.subtract).then_inc(hidden_lo_ready, 1)

            def both_low_part(k):
                pool.wait_ge(both_hi_ready, k + 1)
                if k == 0:
                    pool.wait_ge(down_psum, STEPS)
                if k >= 2:
                    pool.wait_ge(fin_psum, k - 1)
                pool.tensor_tensor(both_lo[:, k % 2, :], both[:, k % 2, :], both_hi[:, k % 2, :].bitcast(F32),
                                   ALU.subtract).then_inc(both_lo_ready, 1)

            root(0)
            root(1)
            wide_low_part(0)
            low_part(0)
            wide_low_part(1)
            wide_low_part(2)
            wide_low_part(3)
            pool.memset(kpad[:, :], 0.0).then_inc(kpad_ready, 1)
            for s in range(STEPS + LAG + 1):
                if SPLIT_LAG <= s < STEPS + SPLIT_LAG:
                    hidden_low_part(s - SPLIT_LAG)
                if s in STATISTICS_AT:
                    root(STATISTICS_AT[s])
                for place in (0, 1):
                    kind, i = job_at(s, place)
                    if kind == "turn":
                        low_part(i)
            for b in range(B - 1):
                both_low_part(b)

        @block.scalar
        def _(act):
            act.preload_act_table(ACT.Exp)
            def high_part(n):
                at = PIECES[n]
                act.wait_ge(wide_loaded[n], 16)
                act.copy(wide_hi[:, at], wide_sb[:, at]).then_inc(wide_hi_ready, 1)

            def take_turned(b):
                act.wait_ge(xt_psum, b + 1)
                if b >= 2:
                    act.wait_ge(logits_psum, b - 1)
                    act.wait_ge(xt_lo_ready, b - 1)
                act.copy(xt_full[:, b % 2, :], ps_side[:, :]).then_inc(xt_full_ready, 1)
                act.copy(xt_hi[:, b, :], ps_side[:, :]).then_inc(xt_hi_ready, 1)

            def exponentials(group):
                b0, n = GROUPS[group]
                act.wait_ge(below_ready, group + 1)
                act.activation(expd[:, b0 * C:(b0 + n) * C, :], below[:, b0 * C:(b0 + n) * C, :],
                               ACT.Exp).then_inc(expd_ready, 1)

            high_part(0)
            take_turned(0)
            act.wait_ge(modes_loaded, 16)
            act.activation(rate[:, :], decay, ACT.Exp).then_inc(decay_exp_ready, 1)
            high_part(1)
            exponentials(0)
            act.wait_ge(rate_ready, 1)
            act.wait_ge(steps_ready, 2)
            act.activation(amp[:, :], steps[:, :], ACT.Exp, scale=rate[:, 0:1]).then_inc(amp_ready, 1)
            high_part(2)
            high_part(3)

            def hidden_high_part(s):
                if s % BLOCKS < SHARED:
                    act.wait_ge(hidden_ready, routed_steps(s) + 1)
                else:
                    act.wait_ge(prod_ready, s + 1)
                if s == SHARED:
                    act.wait_ge(shared_cleared, 1)
                if s >= 3:
                    act.wait_ge(down_psum, s - 2)
                act.copy(hidden_hi[:, s % 3, :], hidden[:, s % BLOCKS, :]).then_inc(hidden_hi_ready, 1)

            def take_down(b):
                act.wait_ge(down_psum, BLOCKS * (b + 1))
                act.activation(g_all[:, b, :], ps_o[:, :], ACT.Silu).then_inc(g_ready, 1)

            def take_inside(k):
                act.wait_ge(inside_psum, k + 1)
                if k >= 2:
                    act.wait_ge(inside_moved[k % 2], 16 * (k // 2))
                act.copy(inside[:, k % 2, :, :],
                         ps_side[:, :].rearrange("p (r i) -> p r i", r=4)[:, :, ::-1]).then_inc(inside_ready, 1)

            def gate_silu(s):
                act.wait_ge(up_psum, s + 1)
                if s >= 2:
                    act.wait_ge(prod_ready, s - 1)
                if s % BLOCKS < SHARED:
                    act.activation(act_g[:, s % 2, :], ps_g[s % 2][:, :], ACT.Silu).then_inc(act_g_ready, 1)
                else:
                    act.activation(act_g[F:P, s % 2, :], ps_g[s % 2][0:F, :], ACT.Silu).then_inc(act_g_ready, 1)

            def turn_parts():
                act.wait_ge(table_ready, 1)
                last = FWD - 1
                act.copy(turn_real[0:N, :], table[0:N, last:last + 1]).then_inc(turn_ready, 1)
                act.copy(turn_real[N:P, :], table[0:N, last:last + 1]).then_inc(turn_ready, 1)
                act.copy(turn_imag[0:N, :], table[N:P, last:last + 1]).then_inc(turn_ready, 1)
                act.mul(turn_imag[N:P, :], table[N:P, last:last + 1], -1.0).then_inc(turn_ready, 1)

            def swap_halves(i):
                c, half = STATES[i]
                at = slice(4 * half, 4 * half + 4)
                act.wait_ge(state_taken, i + 1)
                if followed(i):
                    act.wait_ge(state_ready, followed(i))
                act.copy(swapped[0:N, :, :], state[N:P, c - 1, at, :]).then_inc(swapped_ready, 1)
                act.copy(swapped[N:P, :, :], state[0:N, c - 1, at, :]).then_inc(swapped_ready, 1)

            def job_result(s, place):
                kind, i = job_at(s, place)
                if kind == "turn":
                    take_turned(i)
                if kind == "inside":
                    take_inside(i)

            for s in range(STEPS + LAG + 1):
                if s in G_AT:
                    take_down(G_AT[s])
                if s < STEPS:
                    gate_silu(s)
                job_result(s, 0)
                if s - 1 in BELOW_AT:
                    exponentials(BELOW_AT[s - 1])
                if MODES_AT.get(s - 1) == 2:
                    act.wait_ge(angle_ready, 2)
                    act.wait_ge(consts_ready, 2)
                    act.activation(trig[0:N, :], phase[0:N, :], ACT.Sin, scale=-1.0,
                                   bias=half_pi[0:N, 0:1]).then_inc(trig_ready, 1)
                    act.activation(trig[N:P, :], phase[N:P, :], ACT.Sin).then_inc(trig_ready, 1)
                if SPLIT_LAG <= s < STEPS + SPLIT_LAG:
                    hidden_high_part(s - SPLIT_LAG)
                job_result(s, 1)
                for place in (0, 1):
                    kind, i = job_at(s - 1, place)
                    if kind == "taps":
                        turn_parts()
                    if kind == "state" and STATES[i][0] < C - 1:
                        swap_halves(i)

            for b in range(B + 1):
                if b < B:
                    act.wait_ge(gate_psum, b + 1)
                    if b >= 2:
                        act.wait_ge(both_ready, b - 1)
                    act.activation(gated[:, b % 2, :], ps_gate[b % 2][:, :], ACT.Gelu,
                                   bias=gate_b).then_inc(gate_ready, 1)
                if b >= 1:
                    act.wait_ge(ss_psum, b)
                    if b >= 3:
                        act.wait_ge(both_ready, b - 2)
                    act.activation(ssg[:, (b - 1) % 2, :], ps_ss[(b - 1) % 2][:, :], ACT.Gelu,
                                   bias=ss_b).then_inc(ssg_ready, 1)
                if 1 <= b < B:
                    k = b - 1
                    act.wait_ge(both_ready, k + 1)
                    if k >= 2:
                        act.wait_ge(fin_psum, k - 1)
                    act.copy(both_hi[:, k % 2, :], both[:, k % 2, :]).then_inc(both_hi_ready, 1)

        @block.vector
        def _(dve):
            done = {}

            def link(ins, s):
                done[s.name] = done.get(s.name, 0) + 1
                ins.then_inc(s, 1)
                dve.wait_ge(s, done[s.name])

            def modes_part(n):
                if n == 0:
                    dve.wait_ge(modes_loaded, 16)
                    dve.wait_ge(steps_ready, 2)
                    link(dve.tensor_scalar(omega[:, :], freq, TWO_PI, None, ALU.mult), mode)
                    link(dve.tensor_scalar(phase[:, :], steps[:, :], omega[:, 0:1], None, ALU.mult), mode)
                    link(dve.tensor_scalar(turns[:, :], phase[:, :], 1.0 / TWO_PI, ROUND, ALU.mult, ALU.add), mode)
                    link(dve.tensor_scalar(turns[:, :], turns[:, :], ROUND, None, ALU.subtract), mode)
                elif n == 1:
                    for tp in (TP1, TP2, TP3):
                        link(dve.scalar_tensor_tensor(phase[:, :], turns[:, :], -tp, phase[:, :],
                                                      ALU.mult, ALU.add), mode)
                elif n == 2:
                    link(dve.tensor_scalar(phase[:, :], phase[:, :], PI_BELOW, -PI_BELOW, ALU.min, ALU.max), mode)
                    dve.scalar_tensor_tensor(turns[0:N, :], phase[0:N, :], -1.0, phase[0:N, :], ALU.mult,
                                             ALU.max).then_inc(angle_ready, 1)
                    dve.wait_ge(angle_ready, 1)
                    dve.tensor_copy(phase[0:N, :], turns[0:N, :]).then_inc(angle_ready, 1)
                else:
                    dve.tensor_tensor(mix[:, :], part(modes_sb, MODE_COLS, "in"), part(modes_sb, MODE_COLS, "out"),
                                      ALU.mult).then_inc(mix_ready, 1)
                    dve.wait_ge(mix_ready, 1)
                    dve.tensor_scalar(mix_signed[:, :], mix[:, :], sign, None, ALU.mult).then_inc(mix_ready, 1)
                    dve.wait_ge(trig_ready, 2)
                    dve.wait_ge(amp_ready, 1)
                    dve.tensor_tensor(table[:, :], amp[:, :], trig[:, :], ALU.mult).then_inc(table_ready, 1)

            def statistics(b):
                dve.wait_ge(x_loaded[b], 16)
                for c in range(C):
                    dve.bn_stats(stats[:, b * C + c, :], x_tok[:, b, c, :]).then_inc(stats_ready, 1)
                dve.wait_ge(stats_ready, C * (b + 1))
                for c in range(C):
                    dve.bn_aggr(moments[:, b * C + c, :], stats[:, b * C + c, :]).then_inc(moments_ready, 1)
                dve.wait_ge(moments_ready, C * (b + 1))
                dve.tensor_scalar(spread[:, b * C:(b + 1) * C], moments[:, b * C:(b + 1) * C, 1], EPS, None,
                                  ALU.add).then_inc(spread_ready, 1)

            def normalise(b):
                dve.wait_ge(rstd_ready, b + 1)
                for c in range(C):
                    t = b * C + c
                    dve.tensor_scalar(xn[:, b, c, :], x_tok[:, b, c, :], moments[:, t, 0:1], rstd[:, t:t + 1],
                                      ALU.subtract, ALU.mult).then_inc(xn_ready, 1)

            def take_logits(b):
                dve.wait_ge(logits_psum, b + 1)
                dve.tensor_copy(logits[:, b * C:(b + 1) * C, :].rearrange("p t e -> p (t e)"),
                                ps_side[:, 0:C * E]).then_inc(logits_taken, 1)

            def views(group):
                b0, n = GROUPS[group]
                tiles = slice(b0 * C, (b0 + n) * C)
                return (tiles, lambda t: t[:, tiles, :],
                        lambda t: t[:, tiles].unsqueeze(2).to_broadcast([P, n * C, E]))

            def router_below(group):
                tiles, v, each = views(group)
                dve.wait_ge(logits_taken, sum(GROUPS[group]))
                link(dve.tensor_reduce(top[:, tiles], v(logits), AX, ALU.max), route)
                dve.tensor_tensor(v(below), v(logits), each(top), ALU.subtract).then_inc(below_ready, 1)

            def router_pick(group):
                tiles, v, each = views(group)
                dve.wait_ge(below_ready, group + 1)
                link(dve.scalar_tensor_tensor(v(key), v(below), 0.0, v(rank), ALU.is_ge, ALU.mult), route)
                link(dve.tensor_reduce(best[:, tiles], v(key), AX, ALU.max), route)
                link(dve.tensor_tensor(v(first), v(key), each(best), ALU.is_equal), route)

            def router_pick_second(group):
                tiles, v, each = views(group)
                link(dve.scalar_tensor_tensor(v(rest), v(first), -BIG, v(below), ALU.mult, ALU.add), route)
                link(dve.tensor_reduce(top[:, tiles], v(rest), AX, ALU.max), route)
                link(dve.tensor_tensor(v(rest), v(rest), each(top), ALU.is_ge), route)
                link(dve.tensor_tensor(v(key), v(rest), v(rank), ALU.mult), route)
                link(dve.tensor_reduce(best[:, tiles], v(key), AX, ALU.max), route)
                link(dve.tensor_tensor(v(second), v(key), each(best), ALU.is_equal), route)
                link(dve.tensor_tensor(v(first), v(first), v(second), ALU.add), route)

            def router_weights(group):
                tiles, v, each = views(group)
                dve.wait_ge(expd_ready, group + 1)
                link(dve.tensor_reduce(total[:, tiles], v(expd), AX, ALU.add), route)
                link(dve.reciprocal(rtotal[:, tiles], total[:, tiles]), route)
                link(dve.tensor_tensor(v(weight), v(expd), v(first), ALU.mult), route)
                link(dve.tensor_tensor(v(weight), v(weight), each(rtotal), ALU.mult), route)

            def router_split(group):
                tiles, v, each = views(group)
                link(dve.tensor_copy(parts[:, tiles, 0, :], v(weight)), route)
                link(dve.tensor_tensor(v(remain), v(weight), parts[:, tiles, 0, :], ALU.subtract), route)
                link(dve.tensor_copy(parts[:, tiles, 1, :], v(remain)), route)
                link(dve.tensor_tensor(v(remain), v(remain), parts[:, tiles, 1, :], ALU.subtract), route)
                dve.tensor_copy(parts[:, tiles, 2, :], v(remain)).then_inc(parts_ready, 1)

            dve.memset(parts[:, :, 3, :], 0.0).then_inc(parts_cleared, 1)
            dve.memset(hidden[0:F, SHARED, :], 0.0).then_inc(shared_cleared, 1)
            dve.wait_ge(rank_ready, 1)
            link(dve.tensor_copy(rank[:, :, :], ranki[:, :, :]), route)
            statistics(0)
            statistics(1)
            normalise(0)
            normalise(1)
            take_logits(0)
            router_below(0)
            dve.wait_ge(decay_exp_ready, 1)
            dve.tensor_scalar(rate[:, :], rate[:, :], -1.0, None, ALU.mult).then_inc(rate_ready, 1)
            router_pick(0)
            router_pick_second(0)
            router_weights(0)
            router_split(0)

            for s in range(STEPS + LAG):
                b, j = divmod(s, BLOCKS)

                def product(s):
                    dve.wait_ge(act_g_ready, s + 1)
                    dve.wait_ge(up_psum, s + 1)
                    if s >= BLOCKS:
                        dve.wait_ge(hidden_lo_ready, s - BLOCKS + 1)
                    dve.tensor_tensor(hidden[:, s % BLOCKS, :], act_g[:, s % 2, :], ps_u[s % 2][:, :],
                                      ALU.mult).then_inc(prod_ready, 1)

                def job_result(s, place):
                    kind, i = job_at(s, place)
                    if kind == "route":
                        take_logits(i)
                    if kind == "weights":
                        b0, n = GROUPS[i]
                        dve.wait_ge(weight_psum, i + 1)
                        dve.tensor_copy(weight_t[:, b0:b0 + n, :].rearrange("p b j -> p (b j)"),
                                        ps_side16[:, 0:n * P]).then_inc(weight_t_ready, 1)
                    if kind == "taps":
                        dve.wait_ge(taps_psum, 1)
                        dve.wait_ge(kpad_ready, 1)
                        dve.tensor_copy(kpad[:, 0:P], ps_side[:, 0:P]).then_inc(kpad_ready, 1)
                        dve.tensor_copy(decay_t[:, :], ps_side[:, P:2 * P]).then_inc(decay_t_ready, 1)
                    if kind == "state":
                        c, half = STATES[i]
                        at = slice(4 * half, 4 * half + 4)
                        dve.wait_ge(mix_ready, 2)
                        dve.wait_ge(state_psum, i + 1)
                        added = dve.tensor_tensor(state[:, c - 1, at, :],
                                                  ps_side[:, :].rearrange("m (b h) -> m b h", h=H),
                                                  mix_signed[:, :].unsqueeze(1).to_broadcast([P, 4, H]), ALU.mult)
                        added.then_inc(state_taken, 1)
                        if c > 1:
                            dve.wait_ge(turn_ready, 4)
                            dve.wait_ge(state_taken, i + 1)
                            link(dve.scalar_tensor_tensor(state[:, c - 1, at, :], state[:, c - 2, at, :],
                                                          turn_real[:, 0:1], state[:, c - 1, at, :],
                                                          ALU.mult, ALU.add), chain)
                            dve.wait_ge(swapped_ready, 2 * followed(i))
                            dve.scalar_tensor_tensor(state[:, c - 1, at, :], swapped[:, :, :],
                                                     turn_imag[:, 0:1], state[:, c - 1, at, :],
                                                     ALU.mult, ALU.add).then_inc(state_ready, 1)

                def weigh(s):
                    dve.wait_ge(prod_ready, s + 1)
                    dve.wait_ge(bcast_psum, routed_steps(s) + 1)
                    dve.tensor_tensor(hidden[:, s % BLOCKS, :], hidden[:, s % BLOCKS, :],
                                      ps_w[routed_steps(s) % 2][:, :],
                                      ALU.mult).then_inc(hidden_ready, 1)

                def shared_product(s):
                    dve.wait_ge(act_g_ready, s + 1)
                    if s >= BLOCKS:
                        dve.wait_ge(hidden_lo_ready, s - BLOCKS + 1)
                    dve.tensor_tensor(hidden[F:P, SHARED, :], act_g[F:P, s % 2, :], ps_g[s % 2][F:P, :],
                                      ALU.mult).then_inc(prod_ready, 1)

                if s < STEPS and j < SHARED:
                    product(s)
                if s < STEPS and j == SHARED:
                    shared_product(s)
                job_result(s, 0)
                if SPREAD_LAG <= s < STEPS + SPREAD_LAG and (s - SPREAD_LAG) % BLOCKS < SHARED:
                    weigh(s - SPREAD_LAG)
                job_result(s, 1)
                for kind, i in VECTOR_AT.get(s, []):
                    if kind == "statistics":
                        statistics(i)
                    if kind == "normalise":
                        normalise(i)
                    if kind == "below":
                        router_below(i)
                    if kind == "pick":
                        router_pick(i)
                    if kind == "pick_second":
                        router_pick_second(i)
                    if kind == "weigh":
                        router_weights(i)
                    if kind == "split":
                        router_split(i)
                    if kind == "modes":
                        modes_part(i)

            for b in range(B + 3):
                if b >= 3:
                    k = b - 3
                    dve.wait_ge(fin_psum, k + 1)
                    dve.wait_ge(g_ready, k + 1)
                    if k >= 2:
                        dve.wait_ge(turned_psum, k - 1)
                    dve.scalar_tensor_tensor(scaled[:, k % 2, :], ps_fin[:, :], fin_b, g_all[:, k, :],
                                             ALU.add, ALU.mult).then_inc(scaled_ready, 1)
                if b < B:
                    dve.wait_ge(inter_psum, b + 1)
                    dve.wait_ge(conv_loaded[b], 16)
                    later = conv[:, b, 1:C, :].rearrange("p c i -> p (c i)")
                    dve.tensor_tensor(later, later, ps_inter[b % 2][:, P:L], ALU.add).then_inc(conv_ready, 1)
                if 1 <= b <= B:
                    k = b - 1
                    dve.wait_ge(gate_ready, k + 1)
                    dve.wait_ge(ssg_ready, k + 1)
                    if k == 0:
                        dve.wait_ge(hidden_lo_ready, STEPS)
                    if k >= 2:
                        dve.wait_ge(fin_psum, k - 1)
                    dve.tensor_tensor(both[:, k % 2, :], gated[:, k % 2, :], ssg[:, k % 2, :],
                                      ALU.mult).then_inc(both_ready, 1)
                if b >= 3:
                    k = b - 3
                    dve.wait_ge(turned_psum, k + 1)
                    if k >= 2:
                        dve.wait_ge(y_stored[k % 2], 16 * (k // 2))
                    dve.tensor_tensor(y_out[:, k % 2, :], ps_side[:, :],
                                      x_tok[:, k].rearrange("j c h -> j (c h)"), ALU.add).then_inc(y_ready, 1)

        @block.tensor
        def _(pe):
            def three(ps, hi, lo, b):
                pe.matmul(ps, hi, xt_hi[:, b, :], start=True, stop=False)
                pe.matmul(ps, lo, xt_hi[:, b, :], start=False, stop=False)
                return pe.matmul(ps, hi, xt_lo[:, b, :], start=False, stop=True)

            def turn_tokens(b):
                for c in range(C):
                    pe.wait_ge(xn_ready, C * b + c + 1)
                    mm = pe.transpose(ps_side[:, c * P:(c + 1) * P], xn[:, b, c, :], ident)
                mm.then_inc(xt_psum, 1)

            def route_tokens(b):
                pe.wait_ge(xt_full_ready, b + 1)
                for c in range(C):
                    mm = pe.matmul(ps_side[:, c * E:(c + 1) * E], xt_full[:, b % 2, c * P:(c + 1) * P], router,
                                   start=True, stop=True)
                mm.then_inc(logits_psum, 1)

            def turn_weights(group):
                b0, n = GROUPS[group]
                if group == 0:
                    pe.wait_ge(select_loaded, 32)
                    pe.wait_ge(parts_cleared, 1)
                pe.wait_ge(parts_ready, group + 1)
                for i in range(n):
                    b = b0 + i
                    mm = pe.transpose(ps_side16[:, i * P:(i + 1) * P],
                                      parts[:, b * C:(b + 1) * C, :, :].rearrange("p t k e -> p (t k e)"),
                                      ident16[:, :])
                mm.then_inc(weight_psum, 1)

            def up(s):
                b, j = divmod(s, BLOCKS)
                if b == 0:
                    pe.wait_ge(wide_lo_ready, min(j, 2) + 1)
                pe.wait_ge(xt_lo_ready, b + 1)
                if s >= 2:
                    pe.wait_ge(prod_ready, s - 1)
                mm = three(ps_g[s % 2][:, :], gu(wide_hi, 2 * j), gu(wide_lo, 2 * j), b)
                if j < SHARED:
                    mm = three(ps_u[s % 2][:, :], gu(wide_hi, 2 * j + 1), gu(wide_lo, 2 * j + 1), b)
                mm.then_inc(up_psum, 1)

            def spread_weights(s):
                b, j = divmod(s, BLOCKS)
                for group, (b0, n) in enumerate(GROUPS):
                    if j == 0 and b == b0:
                        pe.wait_ge(weight_t_ready, group + 1)
                r = routed_steps(s)
                if r >= 2:
                    pe.wait_ge(hidden_ready, r - 1)
                for c in range(C):
                    mm = pe.matmul(ps_w[r % 2][:, c * P:(c + 1) * P], select_sb[:, j, c, :], weight_t[:, b, :],
                                   start=True, stop=True)
                mm.then_inc(bcast_psum, 1)

            def down(s):
                b, j = divmod(s, BLOCKS)
                pe.wait_ge(hidden_hi_ready, s + 1)
                if s == 0:
                    pe.wait_ge(wide_lo_ready, len(PIECES))
                if j == 0 and b:
                    pe.wait_ge(g_ready, b)
                lo = F if j == SHARED else 0
                at = slice(wd_at + j * H, wd_at + (j + 1) * H)
                ps = ps_o[:, :]
                pe.matmul(ps, wide_hi[lo:P, at], hidden_hi[lo:P, s % 3, :], start=(j == 0), stop=False)
                pe.matmul(ps, wide_lo[lo:P, at], hidden_hi[lo:P, s % 3, :], start=False, stop=False)
                pe.wait_ge(hidden_lo_ready, s + 1)
                pe.matmul(ps, wide_hi[lo:P, at], hidden_lo[lo:P, s % 3, :], start=False,
                          stop=(j == SHARED)).then_inc(down_psum, 1)

            def taps():
                pe.wait_ge(table_ready, 1)
                pe.wait_ge(mix_ready, 1)
                pe.matmul(ps_side[:, 0:P], mix[0:N, :], table[0:N, TAB - P:TAB], start=True, stop=True)
                pe.transpose(ps_side[:, P:2 * P], table[:, FWD:TAB], ident).then_inc(taps_psum, 1)

            def inside_chunks(k):
                pe.wait_ge(toeplitz_loaded[k % RING], 16 * (k // RING + 1))
                for r in range(4):
                    for q in range(4):
                        u = xn[:, :, :, k * CH + 4 * r + q].rearrange("j b c -> j (b c)")
                        mm = pe.matmul(ps_side[32 * q:32 * q + 32, r * P:(r + 1) * P], u,
                                       toeplitz[:, k % RING, 4 * r + q, :], start=True, stop=True,
                                       skip_group_check=True)
                mm.then_inc(inside_psum, 1)

            def chunk_state(i):
                c, half = STATES[i]
                pe.matmul(ps_side[:, :], decay_t[:, :], xn[:, 4 * half:4 * half + 4, c - 1, :],
                          start=True, stop=True).then_inc(state_psum, 1)

            def do(job):
                if job in ALL_JOBS:
                    bank_free(pe, job)
                kind, i = job
                if kind == "turn":
                    turn_tokens(i)
                if kind == "route":
                    route_tokens(i)
                if kind == "weights":
                    turn_weights(i)
                if kind == "taps":
                    taps()
                if kind == "inside":
                    inside_chunks(i)
                if kind == "state":
                    chunk_state(i)

            pe.wait_ge(early_loaded, 16)
            for job in FIRST_JOBS:
                do(job)
            def gate(b):
                if b < 2:
                    pe.wait_ge(prod_ready, STEPS - 1 + b)
                else:
                    pe.wait_ge(gate_ready, b - 1)
                three(ps_gate[b % 2][:, :], wide_hi[:, gate_at:gate_at + H], wide_lo[:, gate_at:gate_at + H],
                      b).then_inc(gate_psum, 1)

            def inter(b):
                if b == 0:
                    pe.wait_ge(state_taken, len(STATES))
                    pe.wait_ge(state_ready, len(STATES) - 2)
                if b >= 2:
                    pe.wait_ge(conv_ready, b - 1)
                for c in range(1, C):
                    mm = pe.matmul(ps_inter[b % 2][:, c * P:(c + 1) * P], state[:, c - 1, b, :],
                                   table[:, 1:1 + P], start=True, stop=True)
                mm.then_inc(inter_psum, 1)

            def ss(b):
                pe.wait_ge(conv_ready, b + 1)
                if b == 0:
                    pe.wait_ge(hidden_ready, routed_steps(STEPS))
                if b >= 2:
                    pe.wait_ge(ssg_ready, b - 1)
                pe.matmul(ps_ss[b % 2][:, :], ss_w, conv[:, b, :, :].rearrange("p c i -> p (c i)"),
                          start=True, stop=True).then_inc(ss_psum, 1)

            def fin(b):
                if b:
                    pe.wait_ge(scaled_ready, b)
                else:
                    pe.wait_ge(g_ready, B)
                if b < B - 1:
                    hi, lo = (w[:, fin_at:fin_at + H] for w in (wide_hi, wide_lo))
                    pe.wait_ge(both_hi_ready, b + 1)
                    pe.matmul(ps_fin[:, :], hi, both_hi[:, b % 2, :], start=True, stop=False)
                    pe.matmul(ps_fin[:, :], lo, both_hi[:, b % 2, :], start=False, stop=False)
                    pe.wait_ge(both_lo_ready, b + 1)
                    pe.matmul(ps_fin[:, :], hi, both_lo[:, b % 2, :], start=False, stop=True).then_inc(fin_psum, 1)
                else:
                    pe.wait_ge(both_ready, b + 1)
                    pe.matmul(ps_fin[:, :], fin_w, both[:, b % 2, :], start=True, stop=True).then_inc(fin_psum, 1)

            def turn_result(b):
                pe.wait_ge(scaled_ready, b + 1)
                if b:
                    pe.wait_ge(y_ready, b)
                else:
                    bank_free(pe, LAST_JOB)
                for c in range(C):
                    mm = pe.transpose(ps_side[:, c * P:(c + 1) * P], scaled[:, b % 2, c * P:(c + 1) * P], ident)
                mm.then_inc(turned_psum, 1)

            for s in range(STEPS + LAG):
                if s < STEPS:
                    up(s)
                do(job_at(s, 0))
                if SPREAD_LAG <= s < STEPS + SPREAD_LAG and (s - SPREAD_LAG) % BLOCKS < SHARED:
                    spread_weights(s - SPREAD_LAG)
                if s >= LAG:
                    down(s - LAG)
                if s == STEPS:
                    gate(0)
                if s == STEPS + 1:
                    inter(0)
                if s == STEPS + 2:
                    gate(1)
                if s == STEPS + 3:
                    inter(1)
                do(job_at(s, 1))

            for b in range(B + 3):
                if b == 2:
                    ss(1)
                if 2 <= b < B:
                    gate(b)
                    inter(b)
                if 1 <= b <= B and b != 2:
                    ss(b - 1)
                if b == B + 1:
                    fin(B - 1)
                if b >= 3:
                    turn_result(b - 3)
                if 2 <= b <= B:
                    fin(b - 2)


def kernel(**inputs):
    import concourse.bacc as bacc
    from concourse.bass_utils import run_bass_kernel_spmd as run

    a = {name: np.asarray(v) for name, v in inputs.items()}
    f32 = np.float32

    def col(v):
        return v.reshape(-1, 1)

    def twice(v):
        return np.concatenate([v, v], axis=0)

    sign = np.concatenate([np.ones((N, 1), f32), -np.ones((N, 1), f32)])
    modes = np.concatenate([
        col(twice(a["L0_attn_frequencies"])), col(twice(a["L0_attn_decays"])), sign,
        twice(a["L0_attn_in_proj"].T), twice(a["L0_attn_out_proj"])], axis=1)
    early = np.concatenate([np.eye(P, dtype=f32), a["L0_ffn_gate_w"].T], axis=1)
    wg, wu = a["L0_ffn_wg"], a["L0_ffn_wu"]
    gus = []
    for j in range(PAIRS):
        for w in (wg, wu):
            gus.append(w[2 * j:2 * j + 2].reshape(P, H).T)
    gus.append(np.concatenate([a["L0_ffn_sg"], a["L0_ffn_su"]], axis=0).T)
    downs = [a["L0_ffn_wd"][2 * j:2 * j + 2].transpose(0, 2, 1).reshape(P, H) for j in range(PAIRS)]
    downs.append(twice(a["L0_ffn_sd"].T))
    wide = np.concatenate(gus + [a["L0_attn_gate_W"].T, a["L0_attn_fin_W"].T] + downs, axis=1)
    late = np.concatenate([a["L0_attn_ss_W"].T, a["L0_attn_fin_W"].T, col(a["L0_attn_ss_b"]),
                                   col(a["L0_attn_gate_b"]), col(a["L0_attn_fin_b"])], axis=1)
    import ml_dtypes
    bf = ml_dtypes.bfloat16
    select = np.zeros((C, 4, E, PAIRS, C, 2, F), bf)
    for c in range(C):
        for e in range(E):
            select[c, 0:3, e, e // 2, c, e % 2, :] = 1
    arrays = {
        "x": a["L0_attn_x"], "modes": modes, "early": early, "wide": wide, "late": late,
        "ident_bf": np.eye(P, dtype=bf), "select": select.reshape(P, PAIRS, C, P),
    }
    arrays = {k: np.ascontiguousarray(v) for k, v in arrays.items()}
    nc = bacc.Bacc("TRN2", target_bir_lowering=False, num_devices=1)
    args = [nc.dram_tensor(k, v.shape, mybir.dt.from_np(v.dtype), kind="ExternalInput").ap()
            for k, v in arrays.items()]
    out = nc.dram_tensor("out", (B, L, H), F32, kind="ExternalOutput").ap()
    layer(nc, *args, out)
    r = run(nc, [arrays], core_ids=[0])
    return r.results[0]["out"]
```

```python
from contextlib import ExitStack

import numpy as np

import concourse.bass as bass
from concourse import mybir

F32 = mybir.dt.float32
F32R = mybir.dt.float32r
BF16 = mybir.dt.bfloat16
I32 = mybir.dt.int32
ALU = mybir.AluOpType
ACT = mybir.ActivationFunctionType
AX = mybir.AxisListType.X

P = 128
B, L, H = 8, 512, 128
C = L // P
NT = B * C
N = 64
E, F = 8, 64
EPS = 1e-5
PAIRS = E // 2
BLOCKS = PAIRS + 1
SHARED = PAIRS
GU = 2 * PAIRS + 1
RING = 2
SPLITS = 3
QUARTER = P // C
CH = 16

def columns(*parts):
    at, out = 0, {}
    for name, width in parts:
        out[name] = (at, width)
        at += width
    return out, at


MODE_COLS, MODE_W = columns(("freq", 1), ("decay", 1), ("sign", 1), ("in", H), ("out", H))
EARLY_COLS, EARLY_W = columns(("ident", P), ("router", QUARTER))
WIDE_COLS, WIDE_W = columns(("gu", GU * P), ("gate", H), ("fin", H), ("wd", BLOCKS * H))
LATE_COLS, LATE_W = columns(("ss", H), ("fin", H), ("ss_b", 1), ("gate_b", 1), ("fin_b", 1))

TWO_PI = 6.283185307179586
TP1 = 6.25
TP2 = 17.0 / 512.0
TP3 = TWO_PI - TP1 - TP2
ROUND = 1.5 * 2.0 ** 23
PI_BELOW = 3.1415925
BIG = 3.0e38

FWD = P + 1
REV = P
TAB = FWD + REV


def layer(nc, x, modes, early, wide, late, ident_bf, select, out):
    ctx = ExitStack()
    with ctx:
        def sb(name, shape, dt=F32):
            return ctx.enter_context(nc.sbuf_tensor(name, shape, dt))

        def sem(name):
            return ctx.enter_context(nc.semaphore(name))

        x_tok = sb("x_tok", [P, B, C, H])
        modes_sb = sb("modes_sb", [P, MODE_W])
        early_sb = sb("early_sb", [P, EARLY_W])
        state = sb("state", [P, C - 1, B, H])
        wide_sb = state[:, :, :, :].rearrange("p c b h -> p (c b h)")[:, 0:WIDE_W]
        late_sb = sb("late_sb", [P, LATE_W])
        ident16 = sb("ident16", [P, P], BF16)
        select_sb = sb("select_sb", [P, PAIRS, C, P], BF16)
        wide_hi = sb("wide_hi", [P, WIDE_W], F32R)
        wide_lo = sb("wide_lo", [P, WIDE_W], F32R)

        def part(t, cols, name):
            at, width = cols[name]
            return t[:, at:at + width]

        freq = part(modes_sb, MODE_COLS, "freq")
        decay = part(modes_sb, MODE_COLS, "decay")
        sign = part(modes_sb, MODE_COLS, "sign")
        ident = part(early_sb, EARLY_COLS, "ident")
        router = part(early_sb, EARLY_COLS, "router")
        wd_at = WIDE_COLS["wd"][0]
        ss_w = part(late_sb, LATE_COLS, "ss")
        fin_w = part(late_sb, LATE_COLS, "fin")
        ss_b = part(late_sb, LATE_COLS, "ss_b")
        gate_b = part(late_sb, LATE_COLS, "gate_b")
        fin_b = part(late_sb, LATE_COLS, "fin_b")

        def gu(t, block):
            return t[:, block * P:(block + 1) * P]

        gate_at, fin_at = WIDE_COLS["gate"][0], WIDE_COLS["fin"][0]
        PIECES = [slice(0, 2 * P), slice(2 * P, 4 * P), slice(4 * P, GU * P), slice(GU * P, WIDE_W)]

        stats = sb("stats", [P, NT, 6])
        moments = sb("moments", [P, NT, 2])
        half_pi = sb("half_pi", [P, 1])
        minus_half = sb("minus_half", [P, C])
        spread = sb("spread", [P, NT])
        rstd = sb("rstd", [P, NT])
        xn = sb("xn", [P, B, C, H])
        xt_full = sb("xt_full", [P, 2, L])
        xt_hi = sb("xt_hi", [P, B, L], F32R)
        xt_lo = sb("xt_lo", [P, B, L], F32R)

        rank = sb("rank", [P, NT, E])
        ranki = sb("ranki", [P, NT, E], I32)
        logits = sb("logits", [P, NT, E])
        logits_t = sb("logits_t", [P, 2, P])
        top = sb("top", [P, NT])
        below = sb("below", [P, NT, E])
        expd = sb("expd", [P, NT, E])
        total = sb("total", [P, NT])
        rtotal = sb("rtotal", [P, NT])
        key = sb("key", [P, NT, E])
        best = sb("best", [P, NT])
        first = sb("first", [P, NT, E])
        rest = sb("rest", [P, NT, E])
        second = sb("second", [P, NT, E])
        weight = sb("weight", [P, NT, E])
        remain = sb("remain", [P, NT, E])
        parts = sb("parts", [P, NT, 4, E], BF16)
        weight_t = sb("weight_t", [P, B, P], BF16)

        omega = sb("omega", [P, 1])
        rate = sb("rate", [P, 1])
        steps = sb("steps", [P, TAB], I32)
        phase = sb("phase", [P, TAB])
        amp = sb("amp", [P, TAB])
        trig = sb("trig", [P, TAB])
        turns = trig
        table = sb("table", [P, TAB])
        mix = sb("mix", [P, H])
        mix_signed = sb("mix_signed", [P, H])
        decay_t = sb("decay_t", [P, P])
        turn_real = sb("turn_real", [P, 1])
        turn_imag = sb("turn_imag", [P, 1])
        swapped = sb("swapped", [P, B // 2, H])
        kpad = sb("kpad", [P, 2 * P])
        toeplitz = sb("toeplitz", [P, RING, CH, P])
        inside = sb("inside", [P, 2, 4, P])
        conv = xn

        act_g = sb("act_g", [P, 2, L])
        hidden = sb("hidden", [P, BLOCKS, L])
        hidden_hi = sb("hidden_hi", [P, SPLITS, L], F32R)
        hidden_lo = sb("hidden_lo", [P, SPLITS, L], F32R)
        scaled = sb("scaled", [P, 2, L])
        g_all = sb("g_all", [P, B, L])
        gated, ssg, both = act_g, hidden[:, 0:2, :], hidden[:, 2:4, :]
        both_hi, both_lo = hidden_hi, hidden_lo
        y_out = toeplitz[:, 0, 0:8, :].rearrange("p (n r) i -> p n (r i)", n=2)

        k_dram = nc.dram_tensor("k_dram", (P, 2 * P), F32, kind="Internal").ap()

        conv_dram = nc.dram_tensor("conv_dram", (H, NT, P), F32, kind="Internal").ap()

        def bank(name):
            return ctx.enter_context(nc.psum_tensor(name, [P, L], F32))

        ps_g = [bank("ps_g0"), bank("ps_g1")]
        ps_u = [bank("ps_u0"), bank("ps_u1")]
        ps_w = [bank("ps_w0"), bank("ps_w1")]
        ps_side = bank("ps_side")
        ps_o = bank("ps_o")
        ps_gate, ps_inter, ps_ss, ps_fin = ps_g, ps_u, ps_w, ps_o

        def ss_bank(b, at):
            return ps_ss[b % 2] if b < B - 1 else [ps_ss[b % 2], ps_ss[1 - b % 2]][at.start > 0]

        def fin_bank(b, at):
            return ps_fin if b < B - 1 else [ps_gate[1 - b % 2], ps_inter[1 - b % 2]][at.start > 0]

        def turned_bank(b, at):
            return ps_side if b < B - 1 else [ps_gate[b % 2], ps_inter[b % 2]][at.start > 0]

        ps_side16 = ps_side[:, :].bitcast(BF16)

        x_loaded = [sem(f"x_loaded{b}") for b in range(B)]
        modes_loaded, early_loaded = sem("modes_loaded"), sem("early_loaded")
        late_loaded = sem("late_loaded")
        wide_loaded = [sem(f"wide_loaded{i}") for i in range(4)]
        select_loaded = sem("select_loaded")
        consts_ready, steps_ready, rank_ready = sem("consts_ready"), sem("steps_ready"), sem("rank_ready")
        stats_ready, moments_ready, spread_ready = sem("stats_ready"), sem("moments_ready"), sem("spread_ready")
        rstd_ready, xn_ready = sem("rstd_ready"), sem("xn_ready")
        xt_psum, xt_full_ready, xt_hi_ready, xt_lo_ready = (
            sem("xt_psum"), sem("xt_full_ready"), sem("xt_hi_ready"), sem("xt_lo_ready"))
        wide_hi_ready, wide_lo_ready = sem("wide_hi_ready"), sem("wide_lo_ready")
        logits_t_ready, logits_turned = sem("logits_t_ready"), sem("logits_turned")
        logits_psum, below_ready, expd_ready = sem("logits_psum"), sem("below_ready"), sem("expd_ready")
        route_step, mode_step, state_step = sem("route_step"), sem("mode_step"), sem("state_step")
        parts_cleared = sem("parts_cleared")
        shared_cleared = sem("shared_cleared")
        parts_ready, weight_psum, weight_t_ready = sem("parts_ready"), sem("weight_psum"), sem("weight_t_ready")
        rate_ready, amp_ready, angle_ready, trig_ready = (
            sem("rate_ready"), sem("amp_ready"), sem("angle_ready"), sem("trig_ready"))
        decay_exp_ready = sem("decay_exp_ready")
        mix_ready, table_ready, taps_psum = sem("mix_ready"), sem("table_ready"), sem("taps_psum")
        kpad_ready, decay_t_ready, k_stored = sem("kpad_ready"), sem("decay_t_ready"), sem("k_stored")
        toeplitz_loaded = [sem(f"toeplitz_loaded{i}") for i in range(RING)]
        up_psum, act_g_ready, prod_ready = sem("up_psum"), sem("act_g_ready"), sem("prod_ready")
        bcast_psum, hidden_ready, down_psum = sem("bcast_psum"), sem("hidden_ready"), sem("down_psum")
        g_ready = sem("g_ready")
        hidden_hi_ready, hidden_lo_ready = sem("hidden_hi_ready"), sem("hidden_lo_ready")
        both_hi_ready, both_lo_ready = sem("both_hi_ready"), sem("both_lo_ready")
        inside_psum, inside_ready = sem("inside_psum"), sem("inside_ready")
        conv_loaded = [sem(f"conv_loaded{b}") for b in range(B)]
        inside_moved = [sem(f"inside_moved{i}") for i in range(2)]
        state_psum, state_taken, state_ready = sem("state_psum"), sem("state_taken"), sem("state_ready")
        swapped_ready, turn_ready = sem("swapped_ready"), sem("turn_ready")
        gate_psum, gate_ready, inter_psum, conv_ready = (
            sem("gate_psum"), sem("gate_ready"), sem("inter_psum"), sem("conv_ready"))
        ss_psum, ssg_ready, both_ready = sem("ss_psum"), sem("ssg_ready"), sem("both_ready")
        fin_psum, scaled_ready, turned_psum, y_ready = (
            sem("fin_psum"), sem("scaled_ready"), sem("turned_psum"), sem("y_ready"))
        logits_taken = sem("logits_taken")
        y_stored = [sem(f"y_stored{i}") for i in range(2)]

        STEPS = B * BLOCKS

        def routed_steps(s):
            return s // BLOCKS * PAIRS + min(s % BLOCKS, PAIRS)

        STATES = [(c, half) for half in range(2) for c in range(1, C)]
        FIRST_JOBS = [("turn", 0), ("route", 0), ("logits", 0)]
        JOBS_AT = {
            0: [None, ("turn", 1)], 1: [("route", 1), ("weights", 0)], 2: [("logits", 1), ("turn", 2)],
            3: [None, ("route", 2)], 4: [("logits", 2)], 7: [("weights", 1)], 9: [None, ("turn", 3)],
            10: [("route", 3), ("logits", 3)], 11: [None, ("turn", 4)], 12: [("route", 4), ("logits", 4)],
            16: [None, ("weights", 2)], 17: [None, ("taps", 0)], 18: [None, ("state", 0)],
            19: [None, ("turn", 5)], 20: [("route", 5), ("logits", 5)], 21: [("turn", 6), ("route", 6)],
            22: [("state", 1), ("turn", 7)], 23: [("route", 7), ("logits", 6)],
            24: [("inside", 0), ("logits", 7)], 25: [None, ("inside", 1)], 26: [("inside", 2), ("weights", 3)],
            27: [None, ("state", 2)], 28: [("inside", 3), ("state", 3)], 29: [None, ("state", 4)],
            30: [("inside", 4), ("inside", 5)], 33: [("inside", 6)], 34: [("state", 5)], 35: [("inside", 7)],
        }
        LAST_JOB = ("result", 0)
        ALL_JOBS = FIRST_JOBS + [job for s in sorted(JOBS_AT) for job in JOBS_AT[s] if job] + [LAST_JOB]

        def job_at(s, place):
            jobs = JOBS_AT.get(s, [])
            return (jobs[place] if place < len(jobs) else None) or ("", 0)

        GROUPS = [(0, 1), (1, 2), (3, 2), (5, 3)]
        VECTOR_AT = {
            0: [("statistics", 2)], 1: [("modes", 0), ("normalise", 2)],
            4: [("below", 1), ("pick", 1), ("pick_second", 1)], 5: [("weigh", 1), ("split", 1)],
            7: [("statistics", 3)], 8: [("normalise", 3), ("statistics", 4)],
            10: [("normalise", 4), ("modes", 1)], 12: [("below", 2), ("pick", 2), ("pick_second", 2)],
            13: [("weigh", 2)], 14: [("modes", 2), ("split", 2)], 16: [("modes", 3)], 17: [("statistics", 5)],
            18: [("normalise", 5), ("statistics", 6)], 19: [("normalise", 6)], 20: [("statistics", 7)],
            21: [("normalise", 7)],
            24: [("below", 3), ("pick", 3), ("pick_second", 3), ("weigh", 3), ("split", 3)],
        }

        def steps_of(kind):
            return {s: i for s, work in VECTOR_AT.items() for k, i in work if k == kind}

        STATISTICS_AT, BELOW_AT, MODES_AT = steps_of("statistics"), steps_of("below"), steps_of("modes")
        SPREAD_LAG, SPLIT_LAG = 2, 3
        LAG = 5
        G_AT = {b * BLOCKS + SHARED + LAG + 1: b for b in range(B)}

        def pieces(b):
            if b < B - 1:
                return [(b + 1, slice(0, L))]
            return [(B, slice(0, L // 2)), (B + 1, slice(L // 2, L))]

        def followed(i):
            return sum(c > 1 for c, half in STATES[:i + 1])

        def bank_free(eng, job):
            n = ALL_JOBS.index(job)
            if n == 0:
                return
            kind, i = ALL_JOBS[n - 1]
            if kind == "turn":
                eng.wait_ge(xt_hi_ready, i + 1)
            elif kind == "route":
                eng.wait_ge(logits_t_ready, i + 1)
            elif kind == "logits":
                eng.wait_ge(logits_taken, i + 1)
            elif kind == "weights":
                eng.wait_ge(weight_t_ready, i + 1)
            elif kind == "taps":
                eng.wait_ge(kpad_ready, 2)
                eng.wait_ge(decay_t_ready, 1)
            elif kind == "inside":
                eng.wait_ge(inside_ready, i + 1)
            else:
                eng.wait_ge(state_taken, i + 1)

        block = ctx.enter_context(nc.Block())

        @block.sync
        def _(sp):
            for b in range(B):
                sp.dma_start(x_tok[:, b], x[b].rearrange("(c j) h -> j c h", j=P)).then_inc(x_loaded[b], 16)
                if b == 0:
                    sp.dma_start(early_sb[:, :], early).then_inc(early_loaded, 16)
                if b == 1:
                    sp.dma_start(wide_sb[:, PIECES[0]], wide[:, PIECES[0]]).then_inc(wide_loaded[0], 16)
                    sp.dma_start(modes_sb[:, :], modes).then_inc(modes_loaded, 16)
                    for piece in (1, 2, 3):
                        sp.dma_start(wide_sb[:, PIECES[piece]], wide[:, PIECES[piece]]).then_inc(
                            wide_loaded[piece], 16)
                    sp.dma_start(ident16[:, :], ident_bf).then_inc(select_loaded, 16)
                    sp.dma_start(select_sb[:, :, :, :], select).then_inc(select_loaded, 16)
                    sp.dma_start(late_sb[:, :], late).then_inc(late_loaded, 16)
            sp.wait_ge(kpad_ready, 2)
            sp.dma_start(k_dram, kpad[:, :]).then_inc(k_stored, 16)
            sp.wait_ge(k_stored, 16)

            def load_toeplitz(k):
                if k >= RING:
                    sp.wait_ge(inside_psum, k - RING + 1)
                src = bass.AP(k_dram.tensor, k_dram.offset + k * CH * 2 * P, [[1, P], [2 * P, CH], [1, P]])
                sp.dma_start(toeplitz[:, k % RING], src).then_inc(toeplitz_loaded[k % RING], 16)

            for k in range(RING):
                load_toeplitz(k)
            for k in range(B):
                sp.wait_ge(inside_ready, k + 1)
                sp.dma_start(conv_dram[k * CH:(k + 1) * CH].rearrange("(r q) m i -> (q m) r i", q=4),
                             inside[:, k % 2, :, :]).then_inc(inside_moved[k % 2], 16)
                if k + RING < B:
                    load_toeplitz(k + RING)
            for i in range(2):
                sp.wait_ge(inside_moved[i], 16 * (B // 2))
            sp.wait_ge(state_psum, len(STATES))
            for b in range(B):
                sp.dma_start(conv[:, b, :, :], conv_dram[:, b * C:(b + 1) * C, :]).then_inc(conv_loaded[b], 16)
            for b in range(B):
                for n, at in pieces(b):
                    sp.wait_ge(y_ready, n)
                    sp.dma_start(out[b, at].rearrange("(c j) h -> j c h", j=P),
                                 y_out[:, b % 2, at].rearrange("j (c h) -> j c h", h=H)).then_inc(
                                     y_stored[b % 2], 16)
            sp.wait_ge(y_stored[0], 16 * (B // 2))
            sp.wait_ge(y_stored[1], 16 * (B // 2 + 1))

        @block.gpsimd
        def _(pool):
            pool.memset(minus_half[:, :], -0.5).then_inc(consts_ready, 1)
            pool.memset(half_pi[:, :], TWO_PI / 4).then_inc(consts_ready, 1)
            pool.iota(ranki[:, :, :], [[0, NT], [-1, E]], base=E, channel_multiplier=0).then_inc(rank_ready, 1)
            pool.iota(steps[:, 0:FWD], [[1, FWD]], base=0, channel_multiplier=0).then_inc(steps_ready, 1)
            pool.iota(steps[:, FWD:TAB], [[-1, REV]], base=REV - 1, channel_multiplier=0).then_inc(steps_ready, 1)
            pool.wait_ge(consts_ready, 1)

            def root(b):
                pool.wait_ge(spread_ready, b + 1)
                at = slice(b * C, (b + 1) * C)
                pool.tensor_tensor(rstd[:, at], spread[:, at], minus_half[:, :], ALU.pow).then_inc(rstd_ready, 1)

            def low_part(b):
                pool.wait_ge(xt_full_ready, b + 1)
                pool.wait_ge(xt_hi_ready, b + 1)
                pool.tensor_tensor(xt_lo[:, b, :], xt_full[:, b % 2, :], xt_hi[:, b, :].bitcast(F32),
                                   ALU.subtract).then_inc(xt_lo_ready, 1)

            def wide_low_part(n):
                at = PIECES[n]
                pool.wait_ge(wide_hi_ready, n + 1)
                pool.wait_ge(wide_loaded[n], 16)
                pool.tensor_tensor(wide_lo[:, at], wide_sb[:, at], wide_hi[:, at].bitcast(F32),
                                   ALU.subtract).then_inc(wide_lo_ready, 1)

            def hidden_low_part(s):
                pool.wait_ge(hidden_hi_ready, s + 1)
                if s == SHARED:
                    pool.wait_ge(shared_cleared, 1)
                if s >= SPLITS:
                    pool.wait_ge(down_psum, s - SPLITS + 1)
                pool.tensor_tensor(hidden_lo[:, s % SPLITS, :], hidden[:, s % BLOCKS, :],
                                   hidden_hi[:, s % SPLITS, :].bitcast(F32),
                                   ALU.subtract).then_inc(hidden_lo_ready, 1)

            def both_low_part(k):
                pool.wait_ge(both_hi_ready, k + 1)
                if k == 0:
                    pool.wait_ge(down_psum, STEPS)
                if k >= 2:
                    pool.wait_ge(fin_psum, k - 1)
                pool.tensor_tensor(both_lo[:, k % 2, :], both[:, k % 2, :], both_hi[:, k % 2, :].bitcast(F32),
                                   ALU.subtract).then_inc(both_lo_ready, 1)

            root(0)
            root(1)
            wide_low_part(0)
            wide_low_part(1)
            wide_low_part(2)
            wide_low_part(3)
            pool.memset(kpad[:, :], 0.0).then_inc(kpad_ready, 1)
            for s in range(STEPS + LAG + 1):
                if SPLIT_LAG <= s < STEPS + SPLIT_LAG:
                    hidden_low_part(s - SPLIT_LAG)
                if s in STATISTICS_AT:
                    root(STATISTICS_AT[s])
                for place in (0, 1):
                    kind, i = job_at(s, place)
                    if kind == "turn":
                        low_part(i)
            for b in range(B - 1):
                both_low_part(b)

        @block.scalar
        def _(act):
            act.preload_act_table(ACT.Exp)
            def high_part(n):
                at = PIECES[n]
                act.wait_ge(wide_loaded[n], 16)
                act.copy(wide_hi[:, at], wide_sb[:, at]).then_inc(wide_hi_ready, 1)

            def take_turned(b):
                act.wait_ge(xt_psum, b + 1)
                if b >= 2:
                    act.wait_ge(logits_psum, b - 1)
                    act.wait_ge(xt_lo_ready, b - 1)
                act.copy(xt_full[:, b % 2, :], ps_side[:, :]).then_inc(xt_full_ready, 1)
                act.copy(xt_hi[:, b, :], ps_side[:, :]).then_inc(xt_hi_ready, 1)

            def take_logits(b):
                act.wait_ge(logits_psum, b + 1)
                if b >= 2:
                    act.wait_ge(logits_turned, b - 1)
                act.copy(logits_t[:, b % 2, :], ps_side[:, 0:P]).then_inc(logits_t_ready, 1)

            def exponentials(group):
                b0, n = GROUPS[group]
                act.wait_ge(below_ready, group + 1)
                act.activation(expd[:, b0 * C:(b0 + n) * C, :], below[:, b0 * C:(b0 + n) * C, :],
                               ACT.Exp).then_inc(expd_ready, 1)

            high_part(0)
            take_turned(0)
            take_logits(0)
            act.wait_ge(modes_loaded, 16)
            act.activation(rate[:, :], decay, ACT.Exp).then_inc(decay_exp_ready, 1)
            high_part(1)
            exponentials(0)
            act.wait_ge(rate_ready, 1)
            act.wait_ge(steps_ready, 2)
            act.activation(amp[:, :], steps[:, :], ACT.Exp, scale=rate[:, 0:1]).then_inc(amp_ready, 1)
            high_part(2)
            high_part(3)

            def hidden_high_part(s):
                if s % BLOCKS < SHARED:
                    act.wait_ge(hidden_ready, routed_steps(s) + 1)
                else:
                    act.wait_ge(prod_ready, s + 1)
                if s == SHARED:
                    act.wait_ge(shared_cleared, 1)
                if s >= SPLITS:
                    act.wait_ge(down_psum, s - SPLITS + 1)
                act.copy(hidden_hi[:, s % SPLITS, :], hidden[:, s % BLOCKS, :]).then_inc(hidden_hi_ready, 1)

            def take_down(b):
                act.wait_ge(down_psum, BLOCKS * (b + 1))
                act.activation(g_all[:, b, :], ps_o[:, :], ACT.Silu).then_inc(g_ready, 1)

            def take_inside(k):
                act.wait_ge(inside_psum, k + 1)
                if k >= 2:
                    act.wait_ge(inside_moved[k % 2], 16 * (k // 2))
                act.copy(inside[:, k % 2, :, :],
                         ps_side[:, :].rearrange("p (r i) -> p r i", r=4)[:, :, ::-1]).then_inc(inside_ready, 1)

            def gate_silu(s):
                act.wait_ge(up_psum, s + 1)
                if s >= 2:
                    act.wait_ge(prod_ready, s - 1)
                if s % BLOCKS < SHARED:
                    act.activation(act_g[:, s % 2, :], ps_g[s % 2][:, :], ACT.Silu).then_inc(act_g_ready, 1)
                else:
                    act.activation(act_g[F:P, s % 2, :], ps_g[s % 2][0:F, :], ACT.Silu).then_inc(act_g_ready, 1)

            def turn_parts():
                act.wait_ge(table_ready, 1)
                last = FWD - 1
                act.copy(turn_real[0:N, :], table[0:N, last:last + 1]).then_inc(turn_ready, 1)
                act.copy(turn_real[N:P, :], table[0:N, last:last + 1]).then_inc(turn_ready, 1)
                act.copy(turn_imag[0:N, :], table[N:P, last:last + 1]).then_inc(turn_ready, 1)
                act.mul(turn_imag[N:P, :], table[N:P, last:last + 1], -1.0).then_inc(turn_ready, 1)

            def swap_halves(i):
                c, half = STATES[i]
                at = slice(4 * half, 4 * half + 4)
                act.wait_ge(state_taken, i + 1)
                if followed(i):
                    act.wait_ge(state_ready, followed(i))
                act.copy(swapped[0:N, :, :], state[N:P, c - 1, at, :]).then_inc(swapped_ready, 1)
                act.copy(swapped[N:P, :, :], state[0:N, c - 1, at, :]).then_inc(swapped_ready, 1)

            def job_result(s, place):
                kind, i = job_at(s, place)
                if kind == "turn":
                    take_turned(i)
                if kind == "route":
                    take_logits(i)
                if kind == "inside":
                    take_inside(i)

            for s in range(STEPS + LAG + 1):
                if s in G_AT:
                    take_down(G_AT[s])
                if s < STEPS:
                    gate_silu(s)
                job_result(s, 0)
                if s - 1 in BELOW_AT:
                    exponentials(BELOW_AT[s - 1])
                if MODES_AT.get(s - 1) == 2:
                    act.wait_ge(angle_ready, 2)
                    act.wait_ge(consts_ready, 2)
                    act.activation(trig[0:N, :], phase[0:N, :], ACT.Sin, scale=-1.0,
                                   bias=half_pi[0:N, 0:1]).then_inc(trig_ready, 1)
                    act.activation(trig[N:P, :], phase[N:P, :], ACT.Sin).then_inc(trig_ready, 1)
                if SPLIT_LAG <= s < STEPS + SPLIT_LAG:
                    hidden_high_part(s - SPLIT_LAG)
                job_result(s, 1)
                for place in (0, 1):
                    kind, i = job_at(s - 1, place)
                    if kind == "taps":
                        turn_parts()
                    if kind == "state" and STATES[i][0] < C - 1:
                        swap_halves(i)

            act.wait_ge(late_loaded, 16)
            for b in range(B + 1):
                if b < B:
                    act.wait_ge(gate_psum, b + 1)
                    if b >= 2:
                        act.wait_ge(both_ready, b - 1)
                    act.activation(gated[:, b % 2, :], ps_gate[b % 2][:, :], ACT.Gelu,
                                   bias=gate_b).then_inc(gate_ready, 1)
                if b >= 1:
                    k = b - 1
                    if k >= 2:
                        act.wait_ge(both_ready, k - 1)
                    for n, at in pieces(k):
                        act.wait_ge(ss_psum, n)
                        act.activation(ssg[:, k % 2, at], ss_bank(k, at)[:, at], ACT.Gelu,
                                       bias=ss_b).then_inc(ssg_ready, 1)
                if 1 <= b < B:
                    k = b - 1
                    act.wait_ge(both_ready, k + 1)
                    if k >= 2:
                        act.wait_ge(fin_psum, k - 1)
                    act.copy(both_hi[:, k % 2, :], both[:, k % 2, :]).then_inc(both_hi_ready, 1)

        @block.vector
        def _(dve):
            done = {}

            def link(ins, s):
                done[s.name] = done.get(s.name, 0) + 1
                ins.then_inc(s, 1)
                dve.wait_ge(s, done[s.name])

            def modes_part(n):
                if n == 0:
                    dve.wait_ge(modes_loaded, 16)
                    dve.wait_ge(steps_ready, 2)
                    link(dve.tensor_scalar(omega[:, :], freq, TWO_PI, None, ALU.mult), mode_step)
                    link(dve.tensor_scalar(phase[:, :], steps[:, :], omega[:, 0:1], None, ALU.mult), mode_step)
                    link(dve.tensor_scalar(turns[:, :], phase[:, :], 1.0 / TWO_PI, ROUND, ALU.mult, ALU.add),
                         mode_step)
                    link(dve.tensor_scalar(turns[:, :], turns[:, :], ROUND, None, ALU.subtract), mode_step)
                elif n == 1:
                    for tp in (TP1, TP2, TP3):
                        link(dve.scalar_tensor_tensor(phase[:, :], turns[:, :], -tp, phase[:, :],
                                                      ALU.mult, ALU.add), mode_step)
                elif n == 2:
                    link(dve.tensor_scalar(phase[:, :], phase[:, :], PI_BELOW, -PI_BELOW, ALU.min, ALU.max),
                         mode_step)
                    dve.scalar_tensor_tensor(turns[0:N, :], phase[0:N, :], -1.0, phase[0:N, :], ALU.mult,
                                             ALU.max).then_inc(angle_ready, 1)
                    dve.wait_ge(angle_ready, 1)
                    dve.tensor_copy(phase[0:N, :], turns[0:N, :]).then_inc(angle_ready, 1)
                else:
                    dve.tensor_tensor(mix[:, :], part(modes_sb, MODE_COLS, "in"), part(modes_sb, MODE_COLS, "out"),
                                      ALU.mult).then_inc(mix_ready, 1)
                    dve.wait_ge(mix_ready, 1)
                    dve.tensor_scalar(mix_signed[:, :], mix[:, :], sign, None, ALU.mult).then_inc(mix_ready, 1)
                    dve.wait_ge(trig_ready, 2)
                    dve.wait_ge(amp_ready, 1)
                    dve.tensor_tensor(table[:, :], amp[:, :], trig[:, :], ALU.mult).then_inc(table_ready, 1)

            def statistics(b):
                dve.wait_ge(x_loaded[b], 16)
                for c in range(C):
                    dve.bn_stats(stats[:, b * C + c, :], x_tok[:, b, c, :]).then_inc(stats_ready, 1)
                dve.wait_ge(stats_ready, C * (b + 1))
                for c in range(C):
                    dve.bn_aggr(moments[:, b * C + c, :], stats[:, b * C + c, :]).then_inc(moments_ready, 1)
                dve.wait_ge(moments_ready, C * (b + 1))
                dve.tensor_scalar(spread[:, b * C:(b + 1) * C], moments[:, b * C:(b + 1) * C, 1], EPS, None,
                                  ALU.add).then_inc(spread_ready, 1)

            def normalise(b):
                dve.wait_ge(rstd_ready, b + 1)
                for c in range(C):
                    t = b * C + c
                    dve.tensor_scalar(xn[:, b, c, :], x_tok[:, b, c, :], moments[:, t, 0:1], rstd[:, t:t + 1],
                                      ALU.subtract, ALU.mult).then_inc(xn_ready, 1)

            def take_logits(b):
                dve.wait_ge(logits_turned, b + 1)
                dve.tensor_copy(logits[:, b * C:(b + 1) * C, :],
                                ps_side[:, 0:P].rearrange("p (c q) -> p c q", c=C)[:, :, 0:E]).then_inc(
                                    logits_taken, 1)

            def views(group):
                b0, n = GROUPS[group]
                tiles = slice(b0 * C, (b0 + n) * C)
                return (tiles, lambda t: t[:, tiles, :],
                        lambda t: t[:, tiles].unsqueeze(2).to_broadcast([P, n * C, E]))

            def router_below(group):
                tiles, v, each = views(group)
                dve.wait_ge(logits_taken, sum(GROUPS[group]))
                link(dve.tensor_reduce(top[:, tiles], v(logits), AX, ALU.max), route_step)
                dve.tensor_tensor(v(below), v(logits), each(top), ALU.subtract).then_inc(below_ready, 1)

            def router_pick(group):
                tiles, v, each = views(group)
                dve.wait_ge(below_ready, group + 1)
                link(dve.scalar_tensor_tensor(v(key), v(below), 0.0, v(rank), ALU.is_ge, ALU.mult), route_step)
                link(dve.tensor_reduce(best[:, tiles], v(key), AX, ALU.max), route_step)
                link(dve.tensor_tensor(v(first), v(key), each(best), ALU.is_equal), route_step)

            def router_pick_second(group):
                tiles, v, each = views(group)
                link(dve.scalar_tensor_tensor(v(rest), v(first), -BIG, v(below), ALU.mult, ALU.add), route_step)
                link(dve.tensor_reduce(top[:, tiles], v(rest), AX, ALU.max), route_step)
                link(dve.tensor_tensor(v(rest), v(rest), each(top), ALU.is_ge), route_step)
                link(dve.tensor_tensor(v(key), v(rest), v(rank), ALU.mult), route_step)
                link(dve.tensor_reduce(best[:, tiles], v(key), AX, ALU.max), route_step)
                link(dve.tensor_tensor(v(second), v(key), each(best), ALU.is_equal), route_step)
                link(dve.tensor_tensor(v(first), v(first), v(second), ALU.add), route_step)

            def router_weights(group):
                tiles, v, each = views(group)
                dve.wait_ge(expd_ready, group + 1)
                link(dve.tensor_reduce(total[:, tiles], v(expd), AX, ALU.add), route_step)
                link(dve.reciprocal(rtotal[:, tiles], total[:, tiles]), route_step)
                link(dve.tensor_tensor(v(weight), v(expd), v(first), ALU.mult), route_step)
                link(dve.tensor_tensor(v(weight), v(weight), each(rtotal), ALU.mult), route_step)

            def router_split(group):
                tiles, v, each = views(group)
                link(dve.tensor_copy(parts[:, tiles, 0, :], v(weight)), route_step)
                link(dve.tensor_tensor(v(remain), v(weight), parts[:, tiles, 0, :], ALU.subtract), route_step)
                link(dve.tensor_copy(parts[:, tiles, 1, :], v(remain)), route_step)
                link(dve.tensor_tensor(v(remain), v(remain), parts[:, tiles, 1, :], ALU.subtract), route_step)
                dve.tensor_copy(parts[:, tiles, 2, :], v(remain)).then_inc(parts_ready, 1)

            dve.memset(parts[:, :, 3, :], 0.0).then_inc(parts_cleared, 1)
            dve.memset(hidden[0:F, SHARED, :], 0.0).then_inc(shared_cleared, 1)
            dve.wait_ge(rank_ready, 1)
            link(dve.tensor_copy(rank[:, :, :], ranki[:, :, :]), route_step)
            statistics(0)
            statistics(1)
            normalise(0)
            normalise(1)
            dve.wait_ge(xt_full_ready, 1)
            dve.wait_ge(xt_hi_ready, 1)
            dve.tensor_tensor(xt_lo[:, 0, :], xt_full[:, 0, :], xt_hi[:, 0, :].bitcast(F32),
                              ALU.subtract).then_inc(xt_lo_ready, 1)
            take_logits(0)
            router_below(0)
            dve.wait_ge(decay_exp_ready, 1)
            dve.tensor_scalar(rate[:, :], rate[:, :], -1.0, None, ALU.mult).then_inc(rate_ready, 1)
            router_pick(0)
            router_pick_second(0)
            router_weights(0)
            router_split(0)

            for s in range(STEPS + LAG):
                b, j = divmod(s, BLOCKS)

                def product(s):
                    dve.wait_ge(act_g_ready, s + 1)
                    dve.wait_ge(up_psum, s + 1)
                    if s >= BLOCKS:
                        dve.wait_ge(hidden_lo_ready, s - BLOCKS + 1)
                    dve.tensor_tensor(hidden[:, s % BLOCKS, :], act_g[:, s % 2, :], ps_u[s % 2][:, :],
                                      ALU.mult).then_inc(prod_ready, 1)

                def job_result(s, place):
                    kind, i = job_at(s, place)
                    if kind == "logits":
                        take_logits(i)
                    if kind == "weights":
                        b0, n = GROUPS[i]
                        dve.wait_ge(weight_psum, i + 1)
                        dve.tensor_copy(weight_t[:, b0:b0 + n, :].rearrange("p b j -> p (b j)"),
                                        ps_side16[:, 0:n * P]).then_inc(weight_t_ready, 1)
                    if kind == "taps":
                        dve.wait_ge(taps_psum, 1)
                        dve.wait_ge(kpad_ready, 1)
                        dve.tensor_copy(kpad[:, 0:P], ps_side[:, 0:P]).then_inc(kpad_ready, 1)
                        dve.tensor_copy(decay_t[:, :], ps_side[:, P:2 * P]).then_inc(decay_t_ready, 1)
                    if kind == "state":
                        c, half = STATES[i]
                        at = slice(4 * half, 4 * half + 4)
                        dve.wait_ge(mix_ready, 2)
                        dve.wait_ge(state_psum, i + 1)
                        added = dve.tensor_tensor(state[:, c - 1, at, :],
                                                  ps_side[:, :].rearrange("m (b h) -> m b h", h=H),
                                                  mix_signed[:, :].unsqueeze(1).to_broadcast([P, 4, H]), ALU.mult)
                        added.then_inc(state_taken, 1)
                        if c > 1:
                            dve.wait_ge(turn_ready, 4)
                            dve.wait_ge(state_taken, i + 1)
                            link(dve.scalar_tensor_tensor(state[:, c - 1, at, :], state[:, c - 2, at, :],
                                                          turn_real[:, 0:1], state[:, c - 1, at, :],
                                                          ALU.mult, ALU.add), state_step)
                            dve.wait_ge(swapped_ready, 2 * followed(i))
                            dve.scalar_tensor_tensor(state[:, c - 1, at, :], swapped[:, :, :],
                                                     turn_imag[:, 0:1], state[:, c - 1, at, :],
                                                     ALU.mult, ALU.add).then_inc(state_ready, 1)

                def weigh(s):
                    dve.wait_ge(prod_ready, s + 1)
                    dve.wait_ge(bcast_psum, routed_steps(s) + 1)
                    dve.tensor_tensor(hidden[:, s % BLOCKS, :], hidden[:, s % BLOCKS, :],
                                      ps_w[routed_steps(s) % 2][:, :],
                                      ALU.mult).then_inc(hidden_ready, 1)

                def shared_product(s):
                    dve.wait_ge(act_g_ready, s + 1)
                    if s >= BLOCKS:
                        dve.wait_ge(hidden_lo_ready, s - BLOCKS + 1)
                    dve.tensor_tensor(hidden[F:P, SHARED, :], act_g[F:P, s % 2, :], ps_g[s % 2][F:P, :],
                                      ALU.mult).then_inc(prod_ready, 1)

                if s < STEPS and j < SHARED:
                    product(s)
                if s < STEPS and j == SHARED:
                    shared_product(s)
                job_result(s, 0)
                if SPREAD_LAG <= s < STEPS + SPREAD_LAG and (s - SPREAD_LAG) % BLOCKS < SHARED:
                    weigh(s - SPREAD_LAG)
                job_result(s, 1)
                for kind, i in VECTOR_AT.get(s, []):
                    if kind == "statistics":
                        statistics(i)
                    if kind == "normalise":
                        normalise(i)
                    if kind == "below":
                        router_below(i)
                    if kind == "pick":
                        router_pick(i)
                    if kind == "pick_second":
                        router_pick_second(i)
                    if kind == "weigh":
                        router_weights(i)
                    if kind == "split":
                        router_split(i)
                    if kind == "modes":
                        modes_part(i)

            dve.wait_ge(late_loaded, 16)

            def scale(k):
                dve.wait_ge(g_ready, k + 1)
                if k >= 2:
                    dve.wait_ge(turned_psum, k - 1)
                for n, at in pieces(k):
                    dve.wait_ge(fin_psum, n)
                    dve.scalar_tensor_tensor(scaled[:, k % 2, at], fin_bank(k, at)[:, at], fin_b, g_all[:, k, at],
                                             ALU.add, ALU.mult).then_inc(scaled_ready, 1)

            for b in range(B + 3):
                if 3 <= b <= B + 1:
                    scale(b - 3)
                if b == B + 1:
                    scale(B - 1)
                if b < B:
                    dve.wait_ge(inter_psum, b + 1)
                    dve.wait_ge(conv_loaded[b], 16)
                    later = conv[:, b, 1:C, :].rearrange("p c i -> p (c i)")
                    dve.tensor_tensor(later, later, ps_inter[b % 2][:, P:L], ALU.add).then_inc(conv_ready, 1)
                if 1 <= b <= B:
                    k = b - 1
                    dve.wait_ge(gate_ready, k + 1)
                    if k == 0:
                        dve.wait_ge(hidden_lo_ready, STEPS)
                    if k >= 2:
                        dve.wait_ge(fin_psum, k - 1)
                    for n, at in pieces(k):
                        dve.wait_ge(ssg_ready, n)
                        dve.tensor_tensor(both[:, k % 2, at], gated[:, k % 2, at], ssg[:, k % 2, at],
                                          ALU.mult).then_inc(both_ready, 1)
                if b >= 3:
                    k = b - 3
                    if k >= 2:
                        dve.wait_ge(y_stored[k % 2], 16 * (k // 2))
                    for n, at in pieces(k):
                        dve.wait_ge(turned_psum, n)
                        dve.tensor_tensor(y_out[:, k % 2, at], turned_bank(k, at)[:, at],
                                          x_tok[:, k].rearrange("j c h -> j (c h)")[:, at],
                                          ALU.add).then_inc(y_ready, 1)

        @block.tensor
        def _(pe):
            def three(ps, hi, lo, b):
                pe.matmul(ps, hi, xt_hi[:, b, :], start=True, stop=False)
                pe.matmul(ps, lo, xt_hi[:, b, :], start=False, stop=False)
                return pe.matmul(ps, hi, xt_lo[:, b, :], start=False, stop=True)

            def turn_tokens(b):
                for c in range(C):
                    pe.wait_ge(xn_ready, C * b + c + 1)
                    mm = pe.transpose(ps_side[:, c * P:(c + 1) * P], xn[:, b, c, :], ident)
                mm.then_inc(xt_psum, 1)

            def route_tokens(b):
                pe.wait_ge(xt_full_ready, b + 1)
                for c in range(C):
                    mm = pe.matmul(ps_side[c * QUARTER:(c + 1) * QUARTER, 0:P], router,
                                   xt_full[:, b % 2, c * P:(c + 1) * P], start=True, stop=True,
                                   skip_group_check=True)
                mm.then_inc(logits_psum, 1)

            def turn_logits(b):
                pe.wait_ge(logits_t_ready, b + 1)
                pe.transpose(ps_side[:, 0:P], logits_t[:, b % 2, :], ident).then_inc(logits_turned, 1)

            def turn_weights(group):
                b0, n = GROUPS[group]
                if group == 0:
                    pe.wait_ge(select_loaded, 32)
                    pe.wait_ge(parts_cleared, 1)
                pe.wait_ge(parts_ready, group + 1)
                for i in range(n):
                    b = b0 + i
                    mm = pe.transpose(ps_side16[:, i * P:(i + 1) * P],
                                      parts[:, b * C:(b + 1) * C, :, :].rearrange("p t k e -> p (t k e)"),
                                      ident16[:, :])
                mm.then_inc(weight_psum, 1)

            def up(s):
                b, j = divmod(s, BLOCKS)
                if b == 0:
                    pe.wait_ge(wide_lo_ready, min(j, 2) + 1)
                pe.wait_ge(xt_lo_ready, b + 1)
                if s >= 2:
                    pe.wait_ge(prod_ready, s - 1)
                mm = three(ps_g[s % 2][:, :], gu(wide_hi, 2 * j), gu(wide_lo, 2 * j), b)
                if j < SHARED:
                    mm = three(ps_u[s % 2][:, :], gu(wide_hi, 2 * j + 1), gu(wide_lo, 2 * j + 1), b)
                mm.then_inc(up_psum, 1)

            def spread_weights(s):
                b, j = divmod(s, BLOCKS)
                for group, (b0, n) in enumerate(GROUPS):
                    if j == 0 and b == b0:
                        pe.wait_ge(weight_t_ready, group + 1)
                r = routed_steps(s)
                if r >= 2:
                    pe.wait_ge(hidden_ready, r - 1)
                for c in range(C):
                    mm = pe.matmul(ps_w[r % 2][:, c * P:(c + 1) * P], select_sb[:, j, c, :], weight_t[:, b, :],
                                   start=True, stop=True)
                mm.then_inc(bcast_psum, 1)

            def down(s):
                b, j = divmod(s, BLOCKS)
                pe.wait_ge(hidden_hi_ready, s + 1)
                if s == 0:
                    pe.wait_ge(wide_lo_ready, len(PIECES))
                if j == 0 and b:
                    pe.wait_ge(g_ready, b)
                lo = F if j == SHARED else 0
                at = slice(wd_at + j * H, wd_at + (j + 1) * H)
                ps = ps_o[:, :]
                pe.matmul(ps, wide_hi[lo:P, at], hidden_hi[lo:P, s % SPLITS, :], start=(j == 0), stop=False)
                pe.matmul(ps, wide_lo[lo:P, at], hidden_hi[lo:P, s % SPLITS, :], start=False, stop=False)
                pe.wait_ge(hidden_lo_ready, s + 1)
                pe.matmul(ps, wide_hi[lo:P, at], hidden_lo[lo:P, s % SPLITS, :], start=False,
                          stop=(j == SHARED)).then_inc(down_psum, 1)

            def taps():
                pe.wait_ge(table_ready, 1)
                pe.wait_ge(mix_ready, 1)
                pe.matmul(ps_side[:, 0:P], mix[0:N, :], table[0:N, TAB - P:TAB], start=True, stop=True)
                pe.transpose(ps_side[:, P:2 * P], table[:, FWD:TAB], ident).then_inc(taps_psum, 1)

            def inside_chunks(k):
                pe.wait_ge(toeplitz_loaded[k % RING], 16 * (k // RING + 1))
                for r in range(4):
                    for q in range(4):
                        u = xn[:, :, :, k * CH + 4 * r + q].rearrange("j b c -> j (b c)")
                        mm = pe.matmul(ps_side[32 * q:32 * q + 32, r * P:(r + 1) * P], u,
                                       toeplitz[:, k % RING, 4 * r + q, :], start=True, stop=True,
                                       skip_group_check=True)
                mm.then_inc(inside_psum, 1)

            def chunk_state(i):
                c, half = STATES[i]
                pe.matmul(ps_side[:, :], decay_t[:, :], xn[:, 4 * half:4 * half + 4, c - 1, :],
                          start=True, stop=True).then_inc(state_psum, 1)

            def do(job):
                if job in ALL_JOBS:
                    bank_free(pe, job)
                kind, i = job
                if kind == "turn":
                    turn_tokens(i)
                if kind == "route":
                    route_tokens(i)
                if kind == "logits":
                    turn_logits(i)
                if kind == "weights":
                    turn_weights(i)
                if kind == "taps":
                    taps()
                if kind == "inside":
                    inside_chunks(i)
                if kind == "state":
                    chunk_state(i)

            pe.wait_ge(early_loaded, 16)
            for job in FIRST_JOBS:
                do(job)
            def gate(b):
                if b < 2:
                    pe.wait_ge(prod_ready, STEPS - 1 + b)
                else:
                    pe.wait_ge(gate_ready, b - 1)
                three(ps_gate[b % 2][:, :], wide_hi[:, gate_at:gate_at + H], wide_lo[:, gate_at:gate_at + H],
                      b).then_inc(gate_psum, 1)

            def inter(b):
                if b == 0:
                    pe.wait_ge(state_taken, len(STATES))
                    pe.wait_ge(state_ready, len(STATES) - 2)
                if b >= 2:
                    pe.wait_ge(conv_ready, b - 1)
                for c in range(1, C):
                    mm = pe.matmul(ps_inter[b % 2][:, c * P:(c + 1) * P], state[:, c - 1, b, :],
                                   table[:, 1:1 + P], start=True, stop=True)
                mm.then_inc(inter_psum, 1)

            def ss(b):
                pe.wait_ge(conv_ready, b + 1)
                if b == 0:
                    pe.wait_ge(hidden_ready, routed_steps(STEPS))
                if b >= 2:
                    pe.wait_ge(ssg_ready, b - 1)
                for n, at in pieces(b):
                    if at.start:
                        pe.wait_ge(ssg_ready, b)
                    pe.matmul(ss_bank(b, at)[:, at], ss_w, conv[:, b, :, :].rearrange("p c i -> p (c i)")[:, at],
                              start=True, stop=True).then_inc(ss_psum, 1)

            def fin(b):
                if b == B - 1:
                    pe.wait_ge(gate_ready, B - 1)
                    pe.wait_ge(conv_ready, B - 1)
                elif b:
                    pe.wait_ge(scaled_ready, b)
                else:
                    pe.wait_ge(g_ready, B)
                if b < B - 1:
                    hi, lo = (w[:, fin_at:fin_at + H] for w in (wide_hi, wide_lo))
                    pe.wait_ge(both_hi_ready, b + 1)
                    pe.matmul(ps_fin[:, :], hi, both_hi[:, b % 2, :], start=True, stop=False)
                    pe.matmul(ps_fin[:, :], lo, both_hi[:, b % 2, :], start=False, stop=False)
                    pe.wait_ge(both_lo_ready, b + 1)
                    pe.matmul(ps_fin[:, :], hi, both_lo[:, b % 2, :], start=False, stop=True).then_inc(fin_psum, 1)
                else:
                    for n, at in pieces(b):
                        pe.wait_ge(both_ready, n)
                        pe.matmul(fin_bank(b, at)[:, at], fin_w, both[:, b % 2, at], start=True,
                                  stop=True).then_inc(fin_psum, 1)

            def turn_result(b):
                if b == B - 1:
                    pe.wait_ge(gate_ready, B)
                    pe.wait_ge(conv_ready, B)
                elif b:
                    pe.wait_ge(y_ready, b)
                else:
                    bank_free(pe, LAST_JOB)
                for n, at in pieces(b):
                    pe.wait_ge(scaled_ready, n)
                    for t in range(at.start, at.stop, P):
                        mm = pe.transpose(turned_bank(b, at)[:, t:t + P], scaled[:, b % 2, t:t + P], ident)
                    mm.then_inc(turned_psum, 1)

            for s in range(STEPS + LAG):
                if s < STEPS:
                    up(s)
                do(job_at(s, 0))
                if SPREAD_LAG <= s < STEPS + SPREAD_LAG and (s - SPREAD_LAG) % BLOCKS < SHARED:
                    spread_weights(s - SPREAD_LAG)
                if s >= LAG:
                    down(s - LAG)
                if s == STEPS:
                    gate(0)
                if s == STEPS + 1:
                    inter(0)
                if s == STEPS + 2:
                    gate(1)
                if s == STEPS + 3:
                    inter(1)
                do(job_at(s, 1))

            pe.wait_ge(late_loaded, 16)
            for b in range(B + 3):
                if 2 <= b < B:
                    gate(b)
                if 1 <= b <= B:
                    ss(b - 1)
                if b == 3:
                    fin(0)
                if 2 <= b < B:
                    inter(b)
                if b == B + 1:
                    fin(B - 1)
                if b >= 3:
                    turn_result(b - 3)
                if 3 <= b <= B:
                    fin(b - 2)


def kernel(**inputs):
    import concourse.bacc as bacc
    from concourse.bass_utils import run_bass_kernel_spmd as run

    a = {name: np.asarray(v) for name, v in inputs.items()}
    f32 = np.float32

    def col(v):
        return v.reshape(-1, 1)

    def twice(v):
        return np.concatenate([v, v], axis=0)

    sign = np.concatenate([np.ones((N, 1), f32), -np.ones((N, 1), f32)])
    modes = np.concatenate([
        col(twice(a["L0_attn_frequencies"])), col(twice(a["L0_attn_decays"])), sign,
        twice(a["L0_attn_in_proj"].T), twice(a["L0_attn_out_proj"])], axis=1)
    early = np.concatenate([np.eye(P, dtype=f32), a["L0_ffn_gate_w"].T, np.zeros((H, QUARTER - E), f32)], axis=1)
    wg, wu = a["L0_ffn_wg"], a["L0_ffn_wu"]
    gus = []
    for j in range(PAIRS):
        for w in (wg, wu):
            gus.append(w[2 * j:2 * j + 2].reshape(P, H).T)
    gus.append(np.concatenate([a["L0_ffn_sg"], a["L0_ffn_su"]], axis=0).T)
    downs = [a["L0_ffn_wd"][2 * j:2 * j + 2].transpose(0, 2, 1).reshape(P, H) for j in range(PAIRS)]
    downs.append(twice(a["L0_ffn_sd"].T))
    wide = np.concatenate(gus + [a["L0_attn_gate_W"].T, a["L0_attn_fin_W"].T] + downs, axis=1)
    late = np.concatenate([a["L0_attn_ss_W"].T, a["L0_attn_fin_W"].T, col(a["L0_attn_ss_b"]),
                                   col(a["L0_attn_gate_b"]), col(a["L0_attn_fin_b"])], axis=1)
    import ml_dtypes
    bf = ml_dtypes.bfloat16
    select = np.zeros((C, 4, E, PAIRS, C, 2, F), bf)
    for c in range(C):
        for e in range(E):
            select[c, 0:3, e, e // 2, c, e % 2, :] = 1
    arrays = {
        "x": a["L0_attn_x"], "modes": modes, "early": early, "wide": wide, "late": late,
        "ident_bf": np.eye(P, dtype=bf), "select": select.reshape(P, PAIRS, C, P),
    }
    arrays = {k: np.ascontiguousarray(v) for k, v in arrays.items()}
    nc = bacc.Bacc("TRN2", target_bir_lowering=False, num_devices=1)
    args = [nc.dram_tensor(k, v.shape, mybir.dt.from_np(v.dtype), kind="ExternalInput").ap()
            for k, v in arrays.items()]
    out = nc.dram_tensor("out", (B, L, H), F32, kind="ExternalOutput").ap()
    layer(nc, *args, out)
    r = run(nc, [arrays], core_ids=[0])
    return r.results[0]["out"]
```
